# Optimizing a Trainium2 kernel written in Bass

```python
import numpy as np
import jax
import jax.numpy as jnp

def _softmax(x, axis=-1):
    return jax.nn.softmax(x, axis=axis)

def _gelu(x):
    return jax.nn.gelu(x, approximate=True)

def _silu(x):
    return jax.nn.silu(x)

def _sigmoid(x):
    return jax.nn.sigmoid(x)

def _layernorm(x, axis=-1, eps=1e-05):
    m = jnp.mean(x, axis=axis, keepdims=True)
    v = jnp.var(x, axis=axis, keepdims=True)
    return (x - m) / jnp.sqrt(v + eps)

def _scatter_add(tgt, idx, src, axis=0):
    return tgt.at[idx].add(src)

def _segment_sum(src, seg, n):
    return jax.ops.segment_sum(src, seg, n)
kernel_name = 'mk_metaformer_d2_conv_nhwc768_r4_8c67d3'

def setup_inputs(seed: int=0):
    np.random.seed(seed)
    _w = jnp.asarray

    def _rec_inputs():
        import jax
        import jax.numpy as jnp
        _gk = jax.random.key(seed)
        x = -0.0005963 + 1.001 * jax.random.normal(jax.random.fold_in(_gk, 1), (1, 16, 16, 192), jnp.float32)
        return x
    x = _rec_inputs()

    def _L0_conv_setup():
        import jax, jax.numpy as jnp
        import numpy as np
        NUM_HEADS = 12

        def get_rel_pos(q_size, k_size, rel_pos):
            idx = jnp.arange(q_size)[:, None] - jnp.arange(k_size)[None, :] + (k_size - 1)
            return rel_pos[idx]
        key = jax.random.key(seed)
        ks = jax.random.split(key, 7)
        B, H, W, C = (1, 16, 16, 192)
        return {'x': jax.random.normal(ks[0], (B, H, W, C), jnp.float32), 'w_qkv': jax.random.normal(ks[1], (C, 3 * C), jnp.float32) * 0.02, 'b_qkv': jnp.zeros((3 * C,), jnp.float32), 'w_o': jax.random.normal(ks[2], (C, C), jnp.float32) * 0.02, 'b_o': jnp.zeros((C,), jnp.float32), 'rel_pos_h': jax.random.normal(ks[3], (2 * H - 1, C // NUM_HEADS), jnp.float32) * 0.02, 'rel_pos_w': jax.random.normal(ks[4], (2 * W - 1, C // NUM_HEADS), jnp.float32) * 0.02}
    _L0_conv_all = _L0_conv_setup()
    _L0_conv_in = {k: v for k, v in _L0_conv_all.items() if k in ('w_qkv', 'b_qkv', 'w_o', 'b_o', 'rel_pos_h', 'rel_pos_w')}
    del _L0_conv_all

    def _L0_ffn_setup():
        import jax, jax.numpy as jnp
        import numpy as np
        N_EMBD = 192
        NUM_EXPERTS = 8
        TOP_K = 2
        B, T = (8, 512)

        def expert_hiddens():
            ratios = np.logspace(np.log10(2.0), np.log10(8.0), NUM_EXPERTS)
            return [(int(N_EMBD * (8.0 / 3.0) * (r / (8.0 / 3.0))) + 63) // 16 * 16 for r in ratios]

        def _forward(x, router_W, gates, ups, downs):
            Bb, Tt, C = x.shape
            logits = jnp.einsum('btc,ec->bte', x, router_W)
            gate = jax.nn.softmax(logits, axis=-1)
            topk_val, topk_idx = jax.lax.top_k(gate, TOP_K)
            x_flat = x.reshape(Bb * Tt, C)
            idx = topk_idx.reshape(-1, TOP_K)
            val = topk_val.reshape(-1, TOP_K)
            out_flat = jnp.zeros_like(x_flat)
            for e in range(NUM_EXPERTS):
                w = jnp.sum(jnp.where(idx == e, val, 0.0), axis=-1)
                g = x_flat @ gates[e].T
                u = x_flat @ ups[e].T
                h = jax.nn.silu(g) * u @ downs[e].T
                out_flat = out_flat + w[:, None] * h
            return x + out_flat.reshape(Bb, Tt, C)
        key = jax.random.key(seed)
        hiddens = expert_hiddens()
        keys = jax.random.split(key, 2 + 3 * NUM_EXPERTS)
        inp = {}
        inp['x'] = jax.random.normal(keys[0], (B, T, N_EMBD), dtype=jnp.float32)
        inp['router_W'] = jax.random.normal(keys[1], (NUM_EXPERTS, N_EMBD), dtype=jnp.float32) * 0.02
        down_std = 0.02 / np.sqrt(2 * 12)
        for e, h in enumerate(hiddens):
            inp[f'gate_W_{e}'] = jax.random.normal(keys[2 + 3 * e], (h, N_EMBD), dtype=jnp.float32) * 0.02
            inp[f'up_W_{e}'] = jax.random.normal(keys[3 + 3 * e], (h, N_EMBD), dtype=jnp.float32) * 0.02
            inp[f'down_W_{e}'] = jax.random.normal(keys[4 + 3 * e], (N_EMBD, h), dtype=jnp.float32) * down_std
        return inp
    _L0_ffn_all = _L0_ffn_setup()
    _L0_ffn_in = {k: v for k, v in _L0_ffn_all.items() if k in ('router_W', 'gate_W_0', 'gate_W_1', 'gate_W_2', 'gate_W_3', 'gate_W_4', 'gate_W_5', 'gate_W_6', 'gate_W_7', 'up_W_0', 'up_W_1', 'up_W_2', 'up_W_3', 'up_W_4', 'up_W_5', 'up_W_6', 'up_W_7', 'down_W_0', 'down_W_1', 'down_W_2', 'down_W_3', 'down_W_4', 'down_W_5', 'down_W_6', 'down_W_7')}
    del _L0_ffn_all

    def _L1_conv_setup():
        import jax, jax.numpy as jnp
        import numpy as np
        NUM_HEADS = 12
        key = jax.random.key(seed)
        k1, k2, k3 = jax.random.split(key, 3)
        B, H, W, C = (8, 32, 32, 192)
        x = jax.random.normal(k1, (B, H, W, C), dtype=jnp.float32)
        qkv_w = jax.random.normal(k2, (3 * C, C), dtype=jnp.float32) * C ** (-0.5)
        qkv_b = jnp.zeros((3 * C,), dtype=jnp.float32)
        proj_w = jax.random.normal(k3, (C, C), dtype=jnp.float32) * C ** (-0.5)
        proj_b = jnp.zeros((C,), dtype=jnp.float32)
        return {'x': x, 'qkv_w': qkv_w, 'qkv_b': qkv_b, 'proj_w': proj_w, 'proj_b': proj_b}
    _L1_conv_all = _L1_conv_setup()
    _L1_conv_in = {k: v for k, v in _L1_conv_all.items() if k in ('qkv_w', 'qkv_b', 'proj_w', 'proj_b')}
    del _L1_conv_all

    def _L1_ffn_setup():
        import jax, jax.numpy as jnp
        import numpy as np
        N_EXPERTS = 8
        TOP_K = 2
        key = jax.random.key(seed)
        ks = jax.random.split(key, 4)
        B, T, C = (8, 128, 192)
        H = 4 * C
        E = N_EXPERTS
        scale = 0.02
        x = jax.random.normal(ks[0], (B, T, C), dtype=jnp.float32)
        gate_w = jax.random.normal(ks[1], (E, C), dtype=jnp.float32) * scale
        gate_b = jnp.zeros((E,), dtype=jnp.float32)
        w1 = jax.random.normal(ks[2], (E, H, C), dtype=jnp.float32) * scale
        b1 = jnp.zeros((E, H), dtype=jnp.float32)
        w2 = jax.random.normal(ks[3], (E, C, H), dtype=jnp.float32) * scale
        b2 = jnp.zeros((E, C), dtype=jnp.float32)
        return {'x': x, 'gate_w': gate_w, 'gate_b': gate_b, 'w1': w1, 'b1': b1, 'w2': w2, 'b2': b2}
    _L1_ffn_all = _L1_ffn_setup()
    _L1_ffn_in = {k: v for k, v in _L1_ffn_all.items() if k in ('gate_w', 'gate_b', 'w1', 'b1', 'w2', 'b2')}
    del _L1_ffn_all
    return {'x': x, 'L0_conv_w_qkv': _L0_conv_in['w_qkv'], 'L0_conv_b_qkv': _L0_conv_in['b_qkv'], 'L0_conv_w_o': _L0_conv_in['w_o'], 'L0_conv_b_o': _L0_conv_in['b_o'], 'L0_conv_rel_pos_h': _L0_conv_in['rel_pos_h'], 'L0_conv_rel_pos_w': _L0_conv_in['rel_pos_w'], 'L0_ffn_router_W': _L0_ffn_in['router_W'], 'L0_ffn_gate_W_0': _L0_ffn_in['gate_W_0'], 'L0_ffn_gate_W_1': _L0_ffn_in['gate_W_1'], 'L0_ffn_gate_W_2': _L0_ffn_in['gate_W_2'], 'L0_ffn_gate_W_3': _L0_ffn_in['gate_W_3'], 'L0_ffn_gate_W_4': _L0_ffn_in['gate_W_4'], 'L0_ffn_gate_W_5': _L0_ffn_in['gate_W_5'], 'L0_ffn_gate_W_6': _L0_ffn_in['gate_W_6'], 'L0_ffn_gate_W_7': _L0_ffn_in['gate_W_7'], 'L0_ffn_up_W_0': _L0_ffn_in['up_W_0'], 'L0_ffn_up_W_1': _L0_ffn_in['up_W_1'], 'L0_ffn_up_W_2': _L0_ffn_in['up_W_2'], 'L0_ffn_up_W_3': _L0_ffn_in['up_W_3'], 'L0_ffn_up_W_4': _L0_ffn_in['up_W_4'], 'L0_ffn_up_W_5': _L0_ffn_in['up_W_5'], 'L0_ffn_up_W_6': _L0_ffn_in['up_W_6'], 'L0_ffn_up_W_7': _L0_ffn_in['up_W_7'], 'L0_ffn_down_W_0': _L0_ffn_in['down_W_0'], 'L0_ffn_down_W_1': _L0_ffn_in['down_W_1'], 'L0_ffn_down_W_2': _L0_ffn_in['down_W_2'], 'L0_ffn_down_W_3': _L0_ffn_in['down_W_3'], 'L0_ffn_down_W_4': _L0_ffn_in['down_W_4'], 'L0_ffn_down_W_5': _L0_ffn_in['down_W_5'], 'L0_ffn_down_W_6': _L0_ffn_in['down_W_6'], 'L0_ffn_down_W_7': _L0_ffn_in['down_W_7'], 'L1_conv_qkv_w': _L1_conv_in['qkv_w'], 'L1_conv_qkv_b': _L1_conv_in['qkv_b'], 'L1_conv_proj_w': _L1_conv_in['proj_w'], 'L1_conv_proj_b': _L1_conv_in['proj_b'], 'L1_ffn_gate_w': _L1_ffn_in['gate_w'], 'L1_ffn_gate_b': _L1_ffn_in['gate_b'], 'L1_ffn_w1': _L1_ffn_in['w1'], 'L1_ffn_b1': _L1_ffn_in['b1'], 'L1_ffn_w2': _L1_ffn_in['w2'], 'L1_ffn_b2': _L1_ffn_in['b2']}

def reference(x, L0_conv_w_qkv, L0_conv_b_qkv, L0_conv_w_o, L0_conv_b_o, L0_conv_rel_pos_h, L0_conv_rel_pos_w, L0_ffn_router_W, L0_ffn_gate_W_0, L0_ffn_gate_W_1, L0_ffn_gate_W_2, L0_ffn_gate_W_3, L0_ffn_gate_W_4, L0_ffn_gate_W_5, L0_ffn_gate_W_6, L0_ffn_gate_W_7, L0_ffn_up_W_0, L0_ffn_up_W_1, L0_ffn_up_W_2, L0_ffn_up_W_3, L0_ffn_up_W_4, L0_ffn_up_W_5, L0_ffn_up_W_6, L0_ffn_up_W_7, L0_ffn_down_W_0, L0_ffn_down_W_1, L0_ffn_down_W_2, L0_ffn_down_W_3, L0_ffn_down_W_4, L0_ffn_down_W_5, L0_ffn_down_W_6, L0_ffn_down_W_7, L1_conv_qkv_w, L1_conv_qkv_b, L1_conv_proj_w, L1_conv_proj_b, L1_ffn_gate_w, L1_ffn_gate_b, L1_ffn_w1, L1_ffn_b1, L1_ffn_w2, L1_ffn_b2):
    import jax
    import jax.numpy as jnp

    def _L0_conv_ref(x, w_qkv, b_qkv, w_o, b_o, rel_pos_h, rel_pos_w):
        import jax, jax.numpy as jnp
        import numpy as np
        NUM_HEADS = 12

        def get_rel_pos(q_size, k_size, rel_pos):
            idx = jnp.arange(q_size)[:, None] - jnp.arange(k_size)[None, :] + (k_size - 1)
            return rel_pos[idx]
        B, H, W, C = x.shape
        NH = NUM_HEADS
        HD = C // NH
        scale = HD ** (-0.5)
        qkv = x @ w_qkv + b_qkv
        qkv = qkv.reshape(B, H * W, 3, NH, HD)
        qkv = jnp.transpose(qkv, (2, 0, 3, 1, 4)).reshape(3, B * NH, H * W, HD)
        q, k, v = (qkv[0], qkv[1], qkv[2])
        Rh = get_rel_pos(H, H, rel_pos_h)
        Rw = get_rel_pos(W, W, rel_pos_w)
        qr = q.reshape(B * NH, H, W, HD)
        rel_h = jnp.einsum('bhwc,hkc->bhwk', qr, Rh)
        rel_w = jnp.einsum('bhwc,wkc->bhwk', qr, Rw)
        attn = jnp.einsum('bmd,bnd->bmn', q, k) * scale
        attn = attn.reshape(B * NH, H, W, H, W)
        attn = attn + rel_h[:, :, :, :, None] + rel_w[:, :, :, None, :]
        attn = attn.reshape(B * NH, H * W, H * W)
        p = jax.nn.softmax(attn, axis=-1)
        o = jnp.einsum('bmn,bnd->bmd', p, v)
        o = o.reshape(B, NH, H * W, HD)
        o = jnp.transpose(o, (0, 2, 1, 3)).reshape(B, H, W, C)
        return o @ w_o + b_o

    def _L0_ffn_ref(x, router_W, gate_W_0, gate_W_1, gate_W_2, gate_W_3, gate_W_4, gate_W_5, gate_W_6, gate_W_7, up_W_0, up_W_1, up_W_2, up_W_3, up_W_4, up_W_5, up_W_6, up_W_7, down_W_0, down_W_1, down_W_2, down_W_3, down_W_4, down_W_5, down_W_6, down_W_7):
        import jax, jax.numpy as jnp
        import numpy as np
        N_EMBD = 192
        NUM_EXPERTS = 8
        TOP_K = 2
        B, T = (8, 512)

        def expert_hiddens():
            ratios = np.logspace(np.log10(2.0), np.log10(8.0), NUM_EXPERTS)
            return [(int(N_EMBD * (8.0 / 3.0) * (r / (8.0 / 3.0))) + 63) // 16 * 16 for r in ratios]

        def _forward(x, router_W, gates, ups, downs):
            Bb, Tt, C = x.shape
            logits = jnp.einsum('btc,ec->bte', x, router_W)
            gate = jax.nn.softmax(logits, axis=-1)
            topk_val, topk_idx = jax.lax.top_k(gate, TOP_K)
            x_flat = x.reshape(Bb * Tt, C)
            idx = topk_idx.reshape(-1, TOP_K)
            val = topk_val.reshape(-1, TOP_K)
            out_flat = jnp.zeros_like(x_flat)
            for e in range(NUM_EXPERTS):
                w = jnp.sum(jnp.where(idx == e, val, 0.0), axis=-1)
                g = x_flat @ gates[e].T
                u = x_flat @ ups[e].T
                h = jax.nn.silu(g) * u @ downs[e].T
                out_flat = out_flat + w[:, None] * h
            return x + out_flat.reshape(Bb, Tt, C)
        gates = [gate_W_0, gate_W_1, gate_W_2, gate_W_3, gate_W_4, gate_W_5, gate_W_6, gate_W_7]
        ups = [up_W_0, up_W_1, up_W_2, up_W_3, up_W_4, up_W_5, up_W_6, up_W_7]
        downs = [down_W_0, down_W_1, down_W_2, down_W_3, down_W_4, down_W_5, down_W_6, down_W_7]
        return _forward(x, router_W, gates, ups, downs)

    def _L1_conv_ref(x, qkv_w, qkv_b, proj_w, proj_b):
        import jax, jax.numpy as jnp
        import numpy as np
        NUM_HEADS = 12
        B, H, W, C = x.shape
        N = H * W
        h = NUM_HEADS
        d = C // h
        scale = d ** (-0.5)
        xf = x.reshape(B, N, C)
        qkv = (xf @ qkv_w.T + qkv_b).reshape(B, N, 3, h, d).transpose(2, 0, 3, 1, 4)
        q, k, v = (qkv[0], qkv[1], qkv[2])
        scores = jnp.einsum('bhnd,bhmd->bhnm', q, k) * scale
        attn = jax.nn.softmax(scores, axis=-1)
        out = jnp.einsum('bhnm,bhmd->bhnd', attn, v)
        out = out.transpose(0, 2, 1, 3).reshape(B, N, C)
        out = out @ proj_w.T + proj_b
        return out.reshape(B, H, W, C)

    def _L1_ffn_ref(x, gate_w, gate_b, w1, b1, w2, b2):
        import jax, jax.numpy as jnp
        import numpy as np
        N_EXPERTS = 8
        TOP_K = 2
        B, T, C = x.shape
        E = gate_w.shape[0]
        xr = x.reshape(B * T, C)
        N = xr.shape[0]
        logits = xr @ gate_w.T + gate_b
        probs = jax.nn.softmax(logits, axis=-1)
        topv, topi = jax.lax.top_k(probs, TOP_K)
        topv = topv / jnp.sum(topv, axis=-1, keepdims=True)
        tok_w = jnp.zeros((N, E), dtype=xr.dtype).at[jnp.arange(N)[:, None], topi].add(topv)
        out = jnp.zeros((N, C), dtype=xr.dtype)
        for e in range(E):
            h = jax.nn.relu(xr @ w1[e].T + b1[e])
            y = h @ w2[e].T + b2[e]
            out = out + tok_w[:, e:e + 1] * y
        return out.reshape(B, T, C)

    def _gn(v, G=32, eps=1e-05):
        B_, H_, W_, C_ = v.shape
        g = v.reshape(B_, H_, W_, G, C_ // G)
        m = jnp.mean(g, axis=(1, 2, 4), keepdims=True)
        s = jnp.var(g, axis=(1, 2, 4), keepdims=True)
        return ((g - m) / jnp.sqrt(s + eps)).reshape(v.shape)

    def _ln_c(v, eps=1e-06):
        m = jnp.mean(v, axis=-1, keepdims=True)
        s = jnp.var(v, axis=-1, keepdims=True)
        return (v - m) / jnp.sqrt(s + eps)

    def _ln_t(v, eps=1e-05):
        m = jnp.mean(v, axis=-1, keepdims=True)
        s = jnp.var(v, axis=-1, keepdims=True)
        return (v - m) / jnp.sqrt(s + eps)

    def _to_tokens(v):
        B_, H_, W_, C_ = v.shape
        return v.reshape(B_, H_ * W_, C_)

    def _from_tokens(t, like):
        return t.reshape(like.shape)
    x = x + _L0_conv_ref(_ln_c(x), L0_conv_w_qkv, L0_conv_b_qkv, L0_conv_w_o, L0_conv_b_o, L0_conv_rel_pos_h, L0_conv_rel_pos_w)
    t = _to_tokens(x)
    t = t + _L0_ffn_ref(_ln_t(t), L0_ffn_router_W, L0_ffn_gate_W_0, L0_ffn_gate_W_1, L0_ffn_gate_W_2, L0_ffn_gate_W_3, L0_ffn_gate_W_4, L0_ffn_gate_W_5, L0_ffn_gate_W_6, L0_ffn_gate_W_7, L0_ffn_up_W_0, L0_ffn_up_W_1, L0_ffn_up_W_2, L0_ffn_up_W_3, L0_ffn_up_W_4, L0_ffn_up_W_5, L0_ffn_up_W_6, L0_ffn_up_W_7, L0_ffn_down_W_0, L0_ffn_down_W_1, L0_ffn_down_W_2, L0_ffn_down_W_3, L0_ffn_down_W_4, L0_ffn_down_W_5, L0_ffn_down_W_6, L0_ffn_down_W_7)
    x = _from_tokens(t, x)
    x = x + _L1_conv_ref(_ln_c(x), L1_conv_qkv_w, L1_conv_qkv_b, L1_conv_proj_w, L1_conv_proj_b)
    t = _to_tokens(x)
    t = t + _L1_ffn_ref(_ln_t(t), L1_ffn_gate_w, L1_ffn_gate_b, L1_ffn_w1, L1_ffn_b1, L1_ffn_w2, L1_ffn_b2)
    x = _from_tokens(t, x)
    return x

_drawn_inputs = setup_inputs


def setup_inputs(seed=0):
    import zlib

    import numpy as np

    out = dict(_drawn_inputs(seed))
    spreads = {'L0_conv_b_qkv': (0.0, 0.1),
     'L0_conv_b_o': (0.0, 0.1),
     'L1_conv_qkv_b': (0.0, 0.1),
     'L1_conv_proj_b': (0.0, 0.1),
     'L1_ffn_gate_b': (0.0, 0.272),
     'L1_ffn_b1': (0.0, 0.593),
     'L1_ffn_b2': (0.0, 0.34)}
    factors = {'L0_conv_w_qkv': 8.0,
     'L0_conv_rel_pos_h': 8.0,
     'L0_conv_rel_pos_w': 8.0,
     'L0_ffn_router_W': 8.0,
     'L0_ffn_gate_W_0': 8.0,
     'L0_ffn_gate_W_1': 8.0,
     'L0_ffn_gate_W_2': 8.0,
     'L0_ffn_gate_W_3': 8.0,
     'L0_ffn_gate_W_4': 8.0,
     'L0_ffn_gate_W_5': 8.0,
     'L0_ffn_gate_W_6': 8.0,
     'L0_ffn_gate_W_7': 8.0,
     'L0_ffn_up_W_0': 8.0,
     'L0_ffn_up_W_1': 8.0,
     'L0_ffn_up_W_2': 8.0,
     'L0_ffn_up_W_3': 8.0,
     'L0_ffn_up_W_4': 8.0,
     'L0_ffn_up_W_5': 8.0,
     'L0_ffn_up_W_6': 8.0,
     'L0_ffn_up_W_7': 8.0,
     'L0_ffn_down_W_0': 8.0,
     'L0_ffn_down_W_1': 8.0,
     'L0_ffn_down_W_2': 8.0,
     'L0_ffn_down_W_3': 8.0,
     'L0_ffn_down_W_4': 8.0,
     'L0_ffn_down_W_5': 8.0,
     'L0_ffn_down_W_6': 8.0,
     'L0_ffn_down_W_7': 8.0}
    for name, (base, spread) in spreads.items():
        noise = np.random.default_rng([zlib.crc32(name.encode()), seed]).standard_normal(out[name].shape)
        drawn = base * np.exp(spread * noise) if base else spread * noise
        out[name] = jnp.asarray(drawn.astype(out[name].dtype))
    for name, factor in factors.items():
        out[name] = (out[name] * factor).astype(out[name].dtype)
    return out
```

```python
from contextlib import ExitStack

import concourse.bass as bass
from concourse import mybir

P = 128
F32 = mybir.dt.float32
ALU = mybir.AluOpType
ACT = mybir.ActivationFunctionType
AX_X = mybir.AxisListType.X

TOK = 256
TT = TOK // P
GRID = 16
C = 192
CL = C - P
HEADS = 12
HD = C // HEADS
SLOT = 32
HB = P // SLOT
HG = HEADS // HB
QK = HG * P
SCALE = float(HD) ** -0.5
REL = 2 * GRID - 1
REL_W = GRID - 1 + P
E = 8
HID0 = [432, 528, 624, 752, 896, 1088, 1312, 1584]
HID1 = 4 * C
BANK = 512

TILES0 = [-(-h // P) for h in HID0]
SIZE0 = [3 * h + n * C for h, n in zip(HID0, TILES0)]
OFF0 = [sum(SIZE0[:e]) for e in range(E + 1)]
TILES1 = HID1 // P
SIZE1 = HID1 + HID1 // 2 + TILES1 * C
AHEAD1 = 3
W_QK, W_V, W_OUT, W_ROUTER = 0, 2 * QK, 2 * QK + C, 2 * QK + 2 * C
W_END = W_ROUTER + E
B_QK, B_V, B_O, B_GATE = 0, 2 * HG, 2 * HG + C, 2 * HG + 2 * C
B_END = B_GATE + E
LN_EPS = [1e-6, 1e-5, 1e-6, 1e-5]


def metaformer_kernel(nc, x_in, weights_hi, weights_lo, params, rel_in, const_in, experts0, experts1,
                      bias1_in, bias2_in, out):
    with ExitStack() as ctx:
        def sb(name, shape):
            return ctx.enter_context(nc.sbuf_tensor(name, [P] + shape, F32))

        def sem(name):
            return ctx.enter_context(nc.semaphore(name))

        w0 = sb("w0", [OFF0[E]])
        w1 = sb("w1", [AHEAD1 * SIZE1])
        att_hi = sb("att_hi", [W_END])
        att_lo = sb("att_lo", [W_END])
        par = sb("par", [2, B_END])
        rel_t = sb("rel_t", [2, REL_W])
        ident = sb("ident", [P])
        onehot = sb("onehot", [TOK])
        small = sb("small", [3 + E])
        bias1 = sb("bias1", [E * TILES1])
        bias2 = sb("bias2", [C])
        x = sb("x", [TT, C])
        xn = sb("xn", [TT, C + CL])
        xnT = sb("xnT", [2, TOK])
        stats = sb("stats", [TT, 6])
        mean_var = sb("mean_var", [TT, 2])
        var_eps = sb("var_eps", [TT])
        rstd = sb("rstd", [TT])
        qT = sb("qT", [HG, TOK])
        kT = sb("kT", [HG, TOK])
        relT = sb("relT", [HG, TOK])
        v1 = sb("v1", [TT, HEADS, HD + 1])
        neg_max = sb("neg_max", [HEADS, TT])
        probs = sb("probs", [HB, TT, TOK])
        probsT = sb("probsT", [2, TT, TOK])
        o_sum = sb("o_sum", [TT, HEADS])
        o_tok = sb("o_tok", [TT, C])
        oT = sb("oT", [2, TOK])
        hidden = probs
        silu_g = probsT
        acc = sb("acc", [TT, C])
        logit = sb("logit", [TT, E])
        ex = sb("ex", [TT, E])
        gate = sb("gate", [TT, E])
        pick = sb("pick", [4, TT, E])
        tmp = sb("tmp", [TT, E])
        red = sb("red", [8, TT])
        combT = sb("combT", [TOK])

        bank = [ctx.enter_context(nc.psum_tensor(f"bank{i}", [P, BANK], F32)) for i in range(8)]

        x_landed, const_landed, par_landed, rel_landed = (sem(s) for s in ("x_landed", "const_landed", "par_landed", "rel_landed"))
        att_landed = [sem(f"att_landed{i}") for i in range(2)]
        e0_landed = [sem(f"e0_landed{i}") for i in range(E)]
        e1_landed = [sem(f"e1_landed{i}") for i in range(E)]
        bias_landed = sem("bias_landed")
        ones_set = sem("ones_set")
        vec_step, pool_step, act_step = sem("vec_step"), sem("pool_step"), sem("act_step")
        stats_ready, rstd_ready, xn_ready = sem("stats_ready"), sem("rstd_ready"), sem("xn_ready")
        xnT_psum, xnT_act, xnT_vec = sem("xnT_psum"), sem("xnT_act"), sem("xnT_vec")
        q_psum, k_psum, v_psum, rel_psum = sem("q_psum"), sem("k_psum"), sem("v_psum"), sem("rel_psum")
        q_ready, k_ready, v_ready = sem("q_ready"), sem("k_ready"), sem("v_ready")
        rel_half, rel_ready = sem("rel_half"), sem("rel_ready")
        scores_psum, max_ready, probs_ready = sem("scores_psum"), sem("max_ready"), sem("probs_ready")
        probsT_psum, probsT_vec, probsT_act = sem("probsT_psum"), sem("probsT_vec"), sem("probsT_act")
        o_psum, o_ready, oT_psum, oT_ready = sem("o_psum"), sem("o_ready"), sem("oT_psum"), sem("oT_ready")
        proj_psum, x_ready = sem("proj_psum"), sem("x_ready")
        logit_psum, logit_ready, exp_ready = sem("logit_psum"), sem("logit_ready"), sem("exp_ready")
        gate_ready = sem("gate_ready")
        combT_psum, combT_ready, bias2_psum = sem("combT_psum"), sem("combT_ready"), sem("bias2_psum")
        acc_ready = sem("acc_ready")
        gu_psum, silu_ready, hidden_ready, hidden_used = sem("gu_psum"), sem("silu_ready"), sem("hidden_ready"), sem("hidden_used")
        up_psum, relu_vec, relu_act, relu_used = sem("up_psum"), sem("relu_vec"), sem("relu_act"), sem("relu_used")
        y0_added, y1_added = sem("y0_added"), sem("y1_added")
        out_landed = sem("out_landed")

        tiles0 = [(e, t, min(P, HID0[e] - t * P)) for e in range(E) for t in range(TILES0[e])]
        tiles1 = [(e, t) for e in range(E) for t in range(TILES1)]
        RING = HB
        LAG = 2

        def place1(e):
            if e < AHEAD1:
                return w1, e * SIZE1, -1
            at = (e - AHEAD1) * SIZE1
            return w0, at, max(i for i in range(E) if OFF0[i] < at + SIZE1)

        def relu_engine(n):
            return "act" if n % 2 else "vec"

        def wait_relu_done(eng, n):
            if relu_engine(n) == "act":
                eng.wait_ge(relu_act, n // 2 + 1)
            else:
                eng.wait_ge(relu_vec, n // 2 + 1)

        def wait_probsT(eng, n):
            if n % 3 == 2:
                eng.wait_ge(probsT_act, (n + 1) // 3)
            else:
                eng.wait_ge(probsT_vec, n + 1 - (n + 1) // 3)

        block = ctx.enter_context(nc.Block())

        @block.sync
        def _(sp):
            sp.dma_start(x[:], x_in.rearrange("(t p) c -> p t c", p=P)).then_inc(x_landed, 16)
            sp.dma_start(ident[:], const_in[:, 0:P]).then_inc(const_landed, 16)
            sp.dma_start(att_hi[:], weights_hi[0]).then_inc(att_landed[0], 16)
            sp.dma_start(att_lo[0:CL, :], weights_lo[0]).then_inc(att_landed[0], 16)
            sp.dma_start(par[:], params).then_inc(par_landed, 16)
            sp.dma_start(rel_t[:], rel_in).then_inc(rel_landed, 16)
            sp.dma_start(onehot[:], const_in[:, P:P + TOK]).then_inc(rel_landed, 16)
            sp.dma_start(small[:], const_in[:, P + TOK:P + TOK + 3 + E]).then_inc(const_landed, 16)
            sp.dma_start(bias1[:], bias1_in).then_inc(bias_landed, 16)
            sp.dma_start(bias2[0:E, :], bias2_in).then_inc(bias_landed, 16)
            for e in range(E):
                sp.dma_start(w0[:, OFF0[e]:OFF0[e + 1]], experts0[:, OFF0[e]:OFF0[e + 1]]).then_inc(e0_landed[e], 16)
            for e in range(AHEAD1):
                sp.dma_start(w1[:, e * SIZE1:(e + 1) * SIZE1], experts1[:, e]).then_inc(e1_landed[e], 16)
            sp.wait_ge(logit_psum, 1)
            sp.dma_start(att_hi[:], weights_hi[1]).then_inc(att_landed[1], 16)
            sp.dma_start(att_lo[0:CL, :], weights_lo[1]).then_inc(att_landed[1], 16)
            for e in range(AHEAD1, E):
                tensor, at, last = place1(e)
                sp.wait_ge(hidden_used, sum(TILES0[:last + 1]))
                sp.dma_start(tensor[:, at:at + SIZE1], experts1[:, e]).then_inc(e1_landed[e], 16)
            sp.wait_ge(x_ready, 4)
            sp.dma_start(out.rearrange("(t p) c -> p t c", p=P), x[:]).then_inc(out_landed, 16)
            sp.wait_ge(out_landed, 16)

        @block.gpsimd
        def _(pool):
            nc.gpsimd.memset(v1[:, :, :, HD:HD + 1], 1.0).then_inc(ones_set, 1)
            pool.wait_ge(const_landed, 32)
            for n in range(4):
                pool.wait_ge(stats_ready, n + 1)
                nc.gpsimd.tensor_scalar(var_eps[:], mean_var[:, :, 1], LN_EPS[n], None, ALU.add).then_inc(pool_step, 1)
                pool.wait_ge(pool_step, n + 1)
                nc.gpsimd.tensor_tensor(rstd[:], var_eps[:], small[:, 0:1].to_broadcast([P, TT]), ALU.pow).then_inc(rstd_ready, 1)

        @block.scalar
        def _(act):
            def norm_T(n):
                act.wait_ge(xnT_psum, n + 1)
                nc.scalar.copy(xnT[:, 0, :], bank[6][:, 0:TOK]).then_inc(xnT_act, 1)

            head = 0
            act.wait_ge(par_landed, 16)
            for layer in range(2):
                norm_T(2 * layer)
                act.wait_ge(q_psum, layer + 1)
                for g in range(HG):
                    nc.scalar.activation(qT[:, g, :], bank[g // 2][:, (g % 2) * TOK:(g % 2 + 1) * TOK], ACT.Identity,
                                         bias=par[:, layer, B_QK + g:B_QK + g + 1]).then_inc(q_ready, 1)
                if layer == 0:
                    act.wait_ge(rel_psum, 1)
                    for half in range(2):
                        rows = relT[:].rearrange("p g (r c) -> p r g c", c=GRID)[:, 8 * half:8 * half + 8]
                        nc.scalar.activation(rows, bank[5 + half][:, 0:HG * P].rearrange("p (r g c) -> p r g c", r=8, g=HG),
                                             ACT.Copy, scale=small[:, 1:2]).then_inc(rel_half, 1)
                for h in range(HEADS):
                    act.wait_ge(max_ready, head + 1)
                    if head >= HB:
                        act.wait_ge(probsT_psum, head - HB + 1)
                    if h == 0 and layer == 1:
                        act.wait_ge(hidden_used, len(tiles0))
                    for t in range(TT):
                        nc.scalar.activation(probs[:, h % HB, t, :], bank[h % HB][:, t * TOK:(t + 1) * TOK], ACT.Exp,
                                             bias=neg_max[:, h, t:t + 1]).then_inc(probs_ready, 1)
                    if head % 3 == 2:
                        act.wait_ge(probsT_psum, head + 1)
                        if head >= 2:
                            act.wait_ge(o_psum, head - 1)
                        nc.scalar.copy(probsT[:, head % 2], bank[4 + head % 2][:]).then_inc(probsT_act, 1)
                    head += 1
                act.wait_ge(oT_psum, layer + 1)
                nc.scalar.copy(oT[:, 0, :], bank[7][:, 0:TOK]).then_inc(oT_ready, 1)
                nc.scalar.copy(oT[0:CL, 1, :], bank[7][0:CL, TOK:2 * TOK]).then_inc(oT_ready, 1)
                norm_T(2 * layer + 1)
                act.wait_ge(logit_ready, layer + 1)
                nc.scalar.activation(ex[:], logit[:], ACT.Exp).then_inc(exp_ready, 1)
                if layer == 0:
                    act.wait_ge(o_psum, HEADS)
                    for n, (e, t, m) in enumerate(tiles0):
                        act.wait_ge(gu_psum, n + 1)
                        if n >= 2:
                            act.wait_ge(hidden_ready, n - 1)
                        nc.scalar.activation(silu_g[0:m, n % 2, 0, :], bank[2 * (n % 3)][0:m, 0:TOK], ACT.Silu).then_inc(silu_ready, 1)
                else:
                    act.wait_ge(bias_landed, 32)
                    act.wait_ge(probsT_psum, 2 * HEADS)
                    for n, (e, t) in enumerate(tiles1):
                        if relu_engine(n) != "act":
                            continue
                        act.wait_ge(up_psum, n + 1)
                        if n >= RING:
                            act.wait_ge(relu_used, n - RING + 1)
                        nc.scalar.activation(hidden[:, n % RING, 0, :], bank[n % 6][:, 0:TOK], ACT.Relu,
                                             bias=bias1[:, e * TILES1 + t:e * TILES1 + t + 1]).then_inc(relu_act, 1)

        @block.vector
        def _(dve):
            steps = [0]

            def step(ins):
                steps[0] += 1
                ins.then_inc(vec_step, 1)
                dve.wait_ge(vec_step, steps[0])

            def norm(n):
                for t in range(TT):
                    step(nc.vector.bn_stats(stats[:, t, :], x[:, t, :]))
                step(nc.vector.bn_aggr(mean_var[:, 0, :], stats[:, 0, :]))
                nc.vector.bn_aggr(mean_var[:, 1, :], stats[:, 1, :]).then_inc(stats_ready, 1)
                dve.wait_ge(rstd_ready, n + 1)
                for t in range(TT):
                    nc.vector.tensor_scalar(xn[:, t, 0:C], x[:, t, :], mean_var[:, t, 0:1], rstd[:, t:t + 1],
                                            ALU.subtract, ALU.mult).then_inc(xn_ready, 1)
                    nc.vector.tensor_scalar(xn[:, t, C:C + CL], x[:, t, P:C], mean_var[:, t, 0:1], rstd[:, t:t + 1],
                                            ALU.subtract, ALU.mult).then_inc(xn_ready, 1)
                dve.wait_ge(xnT_psum, n + 1)
                nc.vector.tensor_copy(xnT[:, 1, :], bank[7][:, 0:TOK]).then_inc(xnT_vec, 1)

            def attend(layer):
                dve.wait_ge(k_psum, layer + 1)
                for g in range(HG):
                    nc.vector.tensor_scalar(kT[:, g, :], bank[2 + g // 2][:, (g % 2) * TOK:(g % 2 + 1) * TOK],
                                            par[:, layer, B_QK + HG + g:B_QK + HG + g + 1], SCALE,
                                            ALU.add, ALU.mult).then_inc(k_ready, 1)
                dve.wait_ge(v_psum, layer + 1)
                dve.wait_ge(ones_set, 1)
                for t in range(TT):
                    nc.vector.tensor_tensor(v1[:, t, :, 0:HD], bank[4][:, t * C:(t + 1) * C].rearrange("p (h d) -> p h d", d=HD),
                                            par[:, layer, B_V:B_V + C].rearrange("p (h d) -> p h d", d=HD), ALU.add).then_inc(v_ready, 1)
                if layer == 0:
                    dve.wait_ge(rel_psum, 2)
                    dve.wait_ge(rel_half, 2)
                    for half, b in enumerate((7, 0)):
                        for g in range(HG):
                            cols = relT[:, g, :].rearrange("p (r c) -> p c r", c=GRID)[:, 8 * half:8 * half + 8]
                            new = bank[b][:, 0:HG * P].rearrange("p (c g r) -> p c g r", c=8, g=HG)[:, :, g]
                            nc.vector.scalar_tensor_tensor(cols, new, small[:, 2:3], cols, ALU.mult, ALU.add).then_inc(rel_ready, 1)
                for h in range(HEADS + 1):
                    head = layer * HEADS + h
                    if h < HEADS:
                        dve.wait_ge(scores_psum, head + 1)
                        nc.vector.tensor_reduce(neg_max[:, h, :], bank[h % HB][:].rearrange("p (t k) -> p t k", t=TT),
                                                AX_X, ALU.max, negate=True).then_inc(max_ready, 1)
                    if h >= 1 and (head - 1) % 3 != 2:
                        dve.wait_ge(probsT_psum, head)
                        if head >= 3:
                            dve.wait_ge(o_psum, head - 2)
                        nc.vector.tensor_copy(probsT[:, (head - 1) % 2], bank[4 + (head - 1) % 2][:]).then_inc(probsT_vec, 1)
                dve.wait_ge(o_psum, (layer + 1) * HEADS)
                o = bank[6][:, 0:TT * HEADS * (HD + 1)].rearrange("p (t h d) -> p t h d", t=TT, h=HEADS)
                step(nc.vector.reciprocal(o_sum[:], o[:, :, :, HD]))
                for t in range(TT):
                    nc.vector.tensor_tensor(o_tok[:, t, :].rearrange("p (h d) -> p h d", d=HD), o[:, t, :, 0:HD],
                                            o_sum[:, t, :].unsqueeze(2).to_broadcast([P, HEADS, HD]), ALU.mult).then_inc(o_ready, 1)
                    step(nc.vector.tensor_tensor(x[:, t, :], x[:, t, :], par[:, layer, B_O:B_O + C], ALU.add))
                dve.wait_ge(proj_psum, layer + 1)
                for t in range(TT):
                    step(nc.vector.tensor_tensor(x[:, t, :], x[:, t, :], bank[4][:, t * C:(t + 1) * C], ALU.add))

            def bc(a):
                return a.unsqueeze(2).to_broadcast([P, TT, E])

            def route(layer):
                dve.wait_ge(logit_psum, layer + 1)
                lp = bank[5][:, 0:TT * E].rearrange("p (t e) -> p t e", e=E)
                if layer == 0:
                    step(nc.vector.tensor_copy(logit[:], lp))
                else:
                    for t in range(TT):
                        step(nc.vector.tensor_tensor(logit[:, t], lp[:, t], par[:, 1, B_GATE:B_GATE + E], ALU.add))
                step(nc.vector.tensor_reduce(red[:, 0], logit[:], AX_X, ALU.max))
                nc.vector.tensor_tensor(logit[:], logit[:], bc(red[:, 0]), ALU.subtract).then_inc(logit_ready, 1)
                dve.wait_ge(exp_ready, layer + 1)
                step(nc.vector.tensor_reduce(red[:, 1], ex[:], AX_X, ALU.add))
                step(nc.vector.reciprocal(red[:, 2], red[:, 1]))
                step(nc.vector.tensor_tensor(gate[:], ex[:], bc(red[:, 2]), ALU.mult))
                rank = small[:, 3:3 + E].unsqueeze(1).to_broadcast([P, TT, E])
                step(nc.vector.tensor_copy(tmp[:], gate[:]))
                for k in range(2):
                    step(nc.vector.tensor_reduce(red[:, 3], tmp[:], AX_X, ALU.max))
                    step(nc.vector.tensor_tensor(pick[:, 2], tmp[:], bc(red[:, 3]), ALU.is_equal))
                    step(nc.vector.tensor_tensor(pick[:, 2], pick[:, 2], rank, ALU.mult))
                    step(nc.vector.tensor_reduce(red[:, 4], pick[:, 2], AX_X, ALU.max))
                    step(nc.vector.tensor_tensor(pick[:, k], pick[:, 2], bc(red[:, 4]), ALU.is_equal))
                    if k == 0:
                        step(nc.vector.scalar_tensor_tensor(tmp[:], pick[:, 0], -2.0, tmp[:], ALU.mult, ALU.add))
                step(nc.vector.tensor_tensor(pick[:, 3], pick[:, 0], pick[:, 1], ALU.add))
                last = nc.vector.tensor_tensor(gate[:], gate[:], pick[:, 3], ALU.mult)
                if layer == 1:
                    step(last)
                    step(nc.vector.tensor_reduce(red[:, 5], gate[:], AX_X, ALU.add))
                    step(nc.vector.reciprocal(red[:, 6], red[:, 5]))
                    last = nc.vector.tensor_tensor(gate[:], gate[:], bc(red[:, 6]), ALU.mult)
                last.then_inc(gate_ready, 1)
                dve.wait_ge(gate_ready, layer + 1)

            def add_expert(layer, e):
                y_added = (y0_added, y1_added)[layer]
                if layer == 0:
                    dve.wait_ge(hidden_used, sum(TILES0[:e + 1]))
                else:
                    dve.wait_ge(relu_used, TILES1 * (e + 1))
                for t in range(TT):
                    if e >= 1:
                        dve.wait_ge(y_added, TT * (e - 1) + t + 1)
                    nc.vector.scalar_tensor_tensor(acc[:, t, :], bank[6 + e % 2][:, t * C:(t + 1) * C], gate[:, t, e:e + 1],
                                                   acc[:, t, :], ALU.mult, ALU.add).then_inc(y_added, 1)

            dve.wait_ge(x_landed, 16)
            dve.wait_ge(par_landed, 16)
            norm(0)
            dve.wait_ge(const_landed, 32)
            attend(0)
            norm(1)
            dve.wait_ge(xn_ready, 2 * TT * 2)
            step(nc.vector.tensor_tensor(acc[:], x[:], xn[:, :, 0:C], ALU.add))
            route(0)
            dve.wait_ge(probsT_psum, HEADS)
            for n, (e, t, m) in enumerate(tiles0):
                dve.wait_ge(silu_ready, n + 1)
                if n >= RING:
                    dve.wait_ge(hidden_used, n - RING + 1)
                nc.vector.tensor_tensor(hidden[0:m, n % RING, 0, :], silu_g[0:m, n % 2, 0, :],
                                        bank[2 * (n % 3) + 1][0:m, 0:TOK], ALU.mult).then_inc(hidden_ready, 1)
                if t == LAG + 1 and e >= 1:
                    add_expert(0, e - 1)
            add_expert(0, E - 1)
            dve.wait_ge(y0_added, TT * E)
            step(nc.vector.tensor_copy(x[:], acc[:]))
            norm(2)
            attend(1)
            norm(3)
            route(1)
            dve.wait_ge(combT_psum, 1)
            nc.vector.tensor_copy(combT[0:E, :], bank[5][0:E, 128:128 + TOK]).then_inc(combT_ready, 1)
            dve.wait_ge(bias2_psum, 1)
            nc.vector.tensor_tensor(acc[:], x[:], bank[7][:, 0:TT * C].rearrange("p (t c) -> p t c", t=TT), ALU.add).then_inc(acc_ready, 1)
            dve.wait_ge(acc_ready, 1)
            dve.wait_ge(bias_landed, 32)
            for n, (e, t) in enumerate(tiles1):
                if relu_engine(n) == "vec":
                    dve.wait_ge(up_psum, n + 1)
                    if n >= RING:
                        dve.wait_ge(relu_used, n - RING + 1)
                    nc.vector.tensor_scalar(hidden[:, n % RING, 0, :], bank[n % 6][:, 0:TOK],
                                            bias1[:, e * TILES1 + t:e * TILES1 + t + 1], 0.0, ALU.add, ALU.max).then_inc(relu_vec, 1)
                if t == LAG + 1 and e >= 1:
                    add_expert(1, e - 1)
            add_expert(1, E - 1)
            for t in range(TT):
                dve.wait_ge(y1_added, TT * (E - 1) + t + 1)
                nc.vector.tensor_copy(x[:, t, :], acc[:, t, :]).then_inc(x_ready, 2)

        @block.tensor
        def _(pe):
            def norm_T(n):
                pe.wait_ge(xn_ready, 2 * TT * (n + 1))
                if n == 2:
                    pe.wait_ge(y0_added, TT * E)
                for t in range(TT):
                    cols = slice(t * P, (t + 1) * P)
                    nc.tensor.transpose(bank[6][:, cols], xn[:, t, 0:P], ident[:])
                    last = nc.tensor.transpose(bank[7][:, cols], xn[:, t, P:C + CL], ident[:])
                last.then_inc(xnT_psum, 1)
                pe.wait_ge(xnT_act, n + 1)
                pe.wait_ge(xnT_vec, n + 1)

            def project(out_ap, cols):
                nc.tensor.matmul(out_ap, att_hi[:, cols], xnT[:, 0, :], start=True, stop=False)
                return nc.tensor.matmul(out_ap, att_lo[0:CL, cols], xnT[0:CL, 1, :], start=False, stop=True)

            def project_tokens(out_ap, t, cols):
                tok = slice(t * P, (t + 1) * P)
                nc.tensor.matmul(out_ap, xnT[:, 0, tok], att_hi[:, cols], start=True, stop=False)
                return nc.tensor.matmul(out_ap, xnT[0:CL, 1, tok], att_lo[0:CL, cols], start=False, stop=True)

            def scores(layer, g):
                for b in range(HB):
                    head = layer * HEADS + g * HB + b
                    if head >= HB:
                        pe.wait_ge(probs_ready, TT * (head - HB + 1))
                for t in range(TT):
                    tok = slice(t * P, (t + 1) * P)
                    for b in range(HB):
                        rows = slice(SLOT * b, SLOT * b + HD)
                        last = nc.tensor.matmul(bank[b][:, t * TOK:(t + 1) * TOK], qT[rows, g, tok], kT[rows, g, :],
                                                start=True, stop=layer == 1, tile_position=(SLOT * b, 0))
                        if layer == 1 and t == TT - 1:
                            last.then_inc(scores_psum, 1)
                    if layer == 0:
                        for b in range(HB):
                            rows = slice(SLOT * b, SLOT * (b + 1))
                            last = nc.tensor.matmul(bank[b][:, t * TOK:(t + 1) * TOK], relT[rows, g, tok], onehot[rows, :],
                                                    start=False, stop=True, tile_position=(SLOT * b, 0))
                            if t == TT - 1:
                                last.then_inc(scores_psum, 1)

            def turn(layer, h):
                head = layer * HEADS + h
                pe.wait_ge(probs_ready, TT * (head + 1))
                if head >= 2:
                    wait_probsT(pe, head - 2)
                for k in range(TT):
                    for t in range(TT):
                        at = k * TOK + t * P
                        last = nc.tensor.transpose(bank[4 + head % 2][:, at:at + P], probs[:, h % HB, t, k * P:(k + 1) * P], ident[:])
                last.then_inc(probsT_psum, 1)

            def weigh(layer, h):
                head = layer * HEADS + h
                wait_probsT(pe, head)
                for t in range(TT):
                    at = (t * HEADS + h) * (HD + 1)
                    for k in range(TT):
                        last = nc.tensor.matmul(bank[6][:, at:at + HD + 1], probsT[:, head % 2, k, t * P:(t + 1) * P],
                                                v1[:, k, h, :], start=k == 0, stop=k == TT - 1)
                last.then_inc(o_psum, 1)

            def attend(layer):
                pe.wait_ge(att_landed[layer], 32)
                for g in range(HG):
                    last = project(bank[g // 2][:, (g % 2) * TOK:(g % 2 + 1) * TOK], slice(W_QK + g * P, W_QK + (g + 1) * P))
                last.then_inc(q_psum, 1)
                for g in range(HG):
                    last = project(bank[2 + g // 2][:, (g % 2) * TOK:(g % 2 + 1) * TOK],
                                   slice(W_QK + QK + g * P, W_QK + QK + (g + 1) * P))
                last.then_inc(k_psum, 1)
                for t in range(TT):
                    last = project_tokens(bank[4][:, t * C:(t + 1) * C], t, slice(W_V, W_V + C))
                last.then_inc(v_psum, 1)
                pe.wait_ge(q_ready, HG * (layer + 1))
                if layer == 0:
                    pe.wait_ge(rel_landed, 32)
                    for axis, banks in enumerate(((5, 6), (7, 0))):
                        order = "p g (r c) -> p r g c" if axis == 0 else "p g (r c) -> p c g r"
                        lines = qT[:].rearrange(order, c=GRID)
                        for i in range(GRID):
                            window = rel_t[:, axis, GRID - 1 - i:GRID - 1 - i + P]
                            at = (i % 8) * HG * GRID
                            last = nc.tensor.matmul(bank[banks[i // 8]][:, at:at + HG * GRID], window, lines[:, i],
                                                    start=True, stop=True)
                        last.then_inc(rel_psum, 1)
                    pe.wait_ge(rel_ready, 2 * HG)
                pe.wait_ge(k_ready, HG * (layer + 1))
                pe.wait_ge(v_ready, TT * (layer + 1))
                for g in range(HG):
                    scores(layer, g)
                    for b in range(HB):
                        h = g * HB + b
                        turn(layer, h)
                        if h >= 1:
                            weigh(layer, h - 1)
                weigh(layer, HEADS - 1)
                pe.wait_ge(o_ready, TT * (layer + 1))
                for t in range(TT):
                    nc.tensor.transpose(bank[7][:, t * P:(t + 1) * P], o_tok[:, t, 0:P], ident[:])
                    last = nc.tensor.transpose(bank[7][0:CL, TOK + t * P:TOK + (t + 1) * P], o_tok[:, t, P:C], ident[:])
                last.then_inc(oT_psum, 1)
                pe.wait_ge(oT_ready, 2 * (layer + 1))
                for t in range(TT):
                    tok = slice(t * P, (t + 1) * P)
                    nc.tensor.matmul(bank[4][:, t * C:(t + 1) * C], oT[:, 0, tok], att_hi[:, W_OUT:W_OUT + C], start=True, stop=False)
                    last = nc.tensor.matmul(bank[4][:, t * C:(t + 1) * C], oT[0:CL, 1, tok], att_lo[0:CL, W_OUT:W_OUT + C],
                                            start=False, stop=True)
                last.then_inc(proj_psum, 1)

            def router(layer):
                for t in range(TT):
                    last = project_tokens(bank[5][:, t * E:(t + 1) * E], t, slice(W_ROUTER, W_ROUTER + E))
                last.then_inc(logit_psum, 1)

            def down0(n):
                e, t, m = tiles0[n]
                if t == 0 and e >= 2:
                    pe.wait_ge(y0_added, TT * (e - 1))
                pe.wait_ge(hidden_ready, n + 1)
                at = OFF0[e] + 3 * HID0[e] + t * C
                for i in range(TT):
                    last = nc.tensor.matmul(bank[6 + e % 2][:, i * C:(i + 1) * C], hidden[0:m, n % RING, 0, i * P:(i + 1) * P],
                                            w0[0:m, at:at + C], start=t == 0 and i == 0, stop=t == TILES0[e] - 1, skip_group_check=True)
                last.then_inc(hidden_used, 1)

            def down1(n):
                e, t = tiles1[n]
                if t == 0 and e >= 2:
                    pe.wait_ge(y1_added, TT * (e - 1))
                wait_relu_done(pe, n)
                tensor, at, _ = place1(e)
                at += HID1 + HID1 // 2 + t * C
                for i in range(TT):
                    last = nc.tensor.matmul(bank[6 + e % 2][:, i * C:(i + 1) * C], hidden[:, n % RING, 0, i * P:(i + 1) * P],
                                            tensor[:, at:at + C], start=t == 0 and i == 0, stop=t == TILES1 - 1, skip_group_check=True)
                last.then_inc(relu_used, 1)

            pe.wait_ge(const_landed, 32)
            norm_T(0)
            attend(0)
            norm_T(1)
            router(0)
            pe.wait_ge(gate_ready, 1)
            for n, (e, t, m) in enumerate(tiles0):
                if t == 0:
                    pe.wait_ge(e0_landed[e], 16)
                if n >= 3:
                    pe.wait_ge(hidden_ready, n - 2)
                g_bank, u_bank = bank[2 * (n % 3)], bank[2 * (n % 3) + 1]
                h, at = HID0[e], OFF0[e] + t * P
                nc.tensor.matmul(g_bank[0:m, 0:TOK], w0[:, at:at + m], xnT[:, 0, :], start=True, stop=False)
                nc.tensor.matmul(u_bank[0:m, 0:TOK], w0[:, at + h:at + h + m], xnT[:, 0, :], start=True, stop=False)
                nc.tensor.matmul(g_bank[0:m, 0:TOK], w0[0:CL, at + 2 * h:at + 2 * h + m], xnT[0:CL, 1, :], start=False, stop=True)
                nc.tensor.matmul(u_bank[0:m, 0:TOK], w0[CL:P, at + 2 * h:at + 2 * h + m], xnT[CL:P, 1, :], start=False, stop=True,
                                 ).then_inc(gu_psum, 1)
                if n >= LAG:
                    down0(n - LAG)
            for n in range(len(tiles0) - LAG, len(tiles0)):
                down0(n)
            norm_T(2)
            attend(1)
            norm_T(3)
            router(1)
            pe.wait_ge(gate_ready, 2)
            for t in range(TT):
                last = nc.tensor.transpose(bank[5][0:E, P + t * P:P + (t + 1) * P], gate[:, t, :], ident[:])
            last.then_inc(combT_psum, 1)
            pe.wait_ge(combT_ready, 1)
            pe.wait_ge(bias_landed, 32)
            for t in range(TT):
                last = nc.tensor.matmul(bank[7][:, t * C:(t + 1) * C], combT[0:E, t * P:(t + 1) * P], bias2[0:E, :], start=True, stop=True)
            last.then_inc(bias2_psum, 1)
            pe.wait_ge(acc_ready, 1)
            for n, (e, t) in enumerate(tiles1):
                if t == 0:
                    pe.wait_ge(e1_landed[e], 16)
                if n >= 6:
                    wait_relu_done(pe, n - 6)
                tensor, at, _ = place1(e)
                half = CL * (t // (TILES1 // 2))
                lo = at + HID1 + (t % (TILES1 // 2)) * P
                nc.tensor.matmul(bank[n % 6][:, 0:TOK], tensor[:, at + t * P:at + (t + 1) * P], xnT[:, 0, :], start=True, stop=False)
                nc.tensor.matmul(bank[n % 6][:, 0:TOK], tensor[half:half + CL, lo:lo + P], xnT[half:half + CL, 1, :],
                                 start=False, stop=True).then_inc(up_psum, 1)
                if n >= LAG:
                    down1(n - LAG)
            for n in range(len(tiles1) - LAG, len(tiles1)):
                down1(n)


def lay_out(inputs):
    import numpy as np

    f = {k: np.asarray(v) for k, v in inputs.items()}

    def heads_apart(w):
        w = w.reshape(w.shape[0], HG, HB, HD)
        return np.pad(w, ((0, 0), (0, 0), (0, 0), (0, SLOT - HD))).reshape(w.shape[0], QK)

    def layer_weights(qkv, w_out, router):
        q, k, v = qkv[:, 0:C], qkv[:, C:2 * C], qkv[:, 2 * C:3 * C]
        return np.concatenate([heads_apart(q), heads_apart(k), v, w_out, router], axis=1)

    def layer_params(b_qkv, b_out, b_gate):
        apart = heads_apart(b_qkv[None, 0:2 * C].reshape(2, C)).reshape(2 * HG, P).T
        rows = np.concatenate([b_qkv[2 * C:3 * C], b_out, b_gate])
        return np.concatenate([apart, np.broadcast_to(rows, (P, rows.size))], axis=1)

    w = np.stack([
        layer_weights(f["L0_conv_w_qkv"], f["L0_conv_w_o"], f["L0_ffn_router_W"].T),
        layer_weights(f["L1_conv_qkv_w"].T, f["L1_conv_proj_w"].T, f["L1_ffn_gate_w"].T)])
    no_bias = np.zeros((E,), np.float32)
    params = np.stack([layer_params(f["L0_conv_b_qkv"], f["L0_conv_b_o"], no_bias),
                       layer_params(f["L1_conv_qkv_b"], f["L1_conv_proj_b"], f["L1_ffn_gate_b"])], axis=1)

    rel = np.zeros((HB, SLOT, 2, REL_W), np.float32)
    for axis, name in enumerate(("L0_conv_rel_pos_h", "L0_conv_rel_pos_w")):
        for b in range(HB):
            at = SLOT * b + GRID * axis
            rel[b, 0:HD, axis, at:at + REL] = f[name][::-1].T
    key = np.arange(TOK)
    slot = np.arange(P) % SLOT
    onehot = np.where(slot[:, None] < GRID, key // GRID == slot[:, None], key % GRID == slot[:, None] - GRID)
    ranks = np.broadcast_to(np.arange(E, 0, -1), (P, E))
    masks = np.stack([slot < GRID, slot >= GRID], axis=1)
    const = np.concatenate([np.eye(P), onehot, np.full((P, 1), -0.5), masks, ranks], axis=1).astype(np.float32)

    blocks = []
    for e in range(E):
        gate, up, down = f[f"L0_ffn_gate_W_{e}"].T, f[f"L0_ffn_up_W_{e}"].T, f[f"L0_ffn_down_W_{e}"].T
        down = np.pad(down, ((0, TILES0[e] * P - HID0[e]), (0, 0))).reshape(TILES0[e], P, C)
        blocks += [gate[0:P], up[0:P], np.concatenate([gate[P:C], up[P:C]]), down.transpose(1, 0, 2).reshape(P, -1)]
    experts0 = np.concatenate(blocks, axis=1)
    w1 = f["L1_ffn_w1"].transpose(2, 0, 1)
    lo = w1[P:C].reshape(CL, E, 2, HID1 // 2).transpose(2, 0, 1, 3).reshape(P, E, HID1 // 2)
    w2 = f["L1_ffn_w2"].transpose(0, 2, 1).reshape(E, TILES1, P, C).transpose(2, 0, 1, 3).reshape(P, E, TILES1 * C)
    experts1 = np.concatenate([w1[0:P], lo, w2], axis=2)
    arrays = {
        "x": f["x"].reshape(TOK, C), "weights_hi": w[:, 0:P], "weights_lo": w[:, P:C], "params": params,
        "rel": rel.reshape(P, 2, REL_W), "const": const, "experts0": experts0, "experts1": experts1,
        "bias1": f["L1_ffn_b1"].reshape(E * TILES1, P).T, "bias2": f["L1_ffn_b2"],
    }
    return {k: np.ascontiguousarray(v, dtype=np.float32) for k, v in arrays.items()}


def kernel(**inputs):
    import concourse.bacc as bacc
    from concourse.bass_utils import run_bass_kernel_spmd

    nc = bacc.Bacc("TRN2", target_bir_lowering=False, num_devices=1)
    arrays = lay_out(inputs)
    args = [nc.dram_tensor(f"{name}_dram", a.shape, F32, kind="ExternalInput").ap() for name, a in arrays.items()]
    out = nc.dram_tensor("out_dram", (TOK, C), F32, kind="ExternalOutput").ap()
    metaformer_kernel(nc, *args, out)
    result = run_bass_kernel_spmd(nc, [{f"{name}_dram": a for name, a in arrays.items()}], core_ids=[0])
    return result.results[0]["out_dram"].reshape(1, GRID, GRID, C)
```

```python
from contextlib import ExitStack

import concourse.bass as bass
from concourse import mybir

P = 128
F32 = mybir.dt.float32
F32R = mybir.dt.float32r
ALU = mybir.AluOpType
ACT = mybir.ActivationFunctionType
AX_X = mybir.AxisListType.X

TOK = 256
TT = TOK // P
GRID = 16
C = 192
CL = C - P
HEADS = 12
HD = C // HEADS
SLOT = 32
HB = P // SLOT
HG = HEADS // HB
QK = HG * P
SCALE = float(HD) ** -0.5
SLOTS = 96
PASSES = -(-TOK // SLOTS)
RING = 4
LAG = 2
TRING = 3
REL = 2 * GRID - 1
REL_W = GRID - 1 + P
E = 8
HID0 = [432, 528, 624, 752, 896, 1088, 1312, 1584]
HID1 = 4 * C
BANK = 512

TILES0 = [-(-h // P) for h in HID0]
SIZE0 = [3 * h + n * C for h, n in zip(HID0, TILES0)]
OFF0 = [sum(SIZE0[:e]) for e in range(E + 1)]
TILES1 = HID1 // P
SIZE1 = HID1 + HID1 // 2 + TILES1 * C
W_QK, W_V, W_OUT, W_ROUTER = 0, 2 * QK, 2 * QK + C, 2 * QK + 2 * C
W_END = W_ROUTER + E
B_QK, B_V, B_O, B_GATE = 0, 2 * HG, 2 * HG + C, 2 * HG + 2 * C
B_END = B_GATE + E
CONST_W = 3 * P + 4 + E
SCRATCH = TT * E * SLOTS + E * TOK + 2 * E * SLOTS + RING * SLOTS + 2 * SLOTS + 2 * C
LN_EPS = [1e-6, 1e-5, 1e-6, 1e-5]


def metaformer_kernel(nc, x_in, weights_hi, weights_lo, params, rel_in, const_in, experts0, experts1,
                      bias1_in, bias2_in, out):
    with ExitStack() as ctx:
        def sb(name, shape, dtype=F32):
            return ctx.enter_context(nc.sbuf_tensor(name, [P] + shape, dtype))

        def sem(name):
            return ctx.enter_context(nc.semaphore(name))

        w0 = sb("w0", [OFF0[E]])
        att_hi = sb("att_hi", [W_END])
        att_lo = sb("att_lo", [W_END])
        par = sb("par", [2, B_END])
        rel_t = sb("rel_t", [2, REL_W])
        const = sb("const", [CONST_W])
        ident, upper = const[:, 0:P], const[:, P:2 * P]
        places = const[:, 2 * P:2 * P + SLOTS]
        small = const[:, 3 * P:CONST_W]
        ones = sb("ones", [P])
        onehot = sb("onehot", [TOK])
        onehot_r = sb("onehot_r", [TOK], F32R)
        bias1 = sb("bias1", [E * TILES1])
        bias2 = sb("bias2", [C])
        x = sb("x", [TT, C])
        xn = sb("xn", [TT, C + CL])
        xnT = sb("xnT", [2, TOK])
        stats = sb("stats", [TT, 6])
        mean_var = sb("mean_var", [TT, 2])
        var_eps = sb("var_eps", [TT])
        rstd = sb("rstd", [TT])
        parts = sb("parts", [6, HG, TOK], F32R)
        q_round, q_parts, k_hi, k_lo, rel_hi, rel_lo = (parts[:, i] for i in range(6))
        scratch = sb("scratch", [SCRATCH])
        used = [0]

        def carve(n):
            used[0] += n
            return scratch[:, used[0] - n:used[0]]

        qT, kT, relT = (carve(HG * TOK).rearrange("p (g t) -> p g t", g=HG) for _ in range(3))
        v1 = sb("v1", [TT, HEADS, SLOT])
        neg_max = sb("neg_max", [HEADS, TT])
        probs = carve(HB * TT * TOK).rearrange("p (h t k) -> p h t k", h=HB, t=TT)
        probsT = carve(TRING * TT * TOK).rearrange("p (h k t) -> p h k t", h=TRING, k=TT)
        o_sum = sb("o_sum", [TT, HEADS])
        o_tok = sb("o_tok", [TT, C])
        oT = sb("oT", [2, TOK])
        used[0] = 0
        chosen = parts[:].rearrange("p a g t -> p (a g t)")[:, 0:TT * E * SLOTS].rearrange("p (t e s) -> p t e s", t=TT, e=E)
        xn_parts = parts[:].rearrange("p a g t -> p (a g t)")[:, TT * E * SLOTS:TT * E * SLOTS + 2 * TT * (C + CL)]
        xn_hi, xn_lo = (a.rearrange("p (t c) -> p t c", t=TT) for a in (xn_parts[:, 0:TT * (C + CL)], xn_parts[:, TT * (C + CL):]))
        weighted = carve(TT * E * SLOTS).rearrange("p (t e s) -> p t e s", t=TT, e=E)
        weightedT = carve(E * TOK).rearrange("p (e t) -> p e t", e=E)
        xe = carve(2 * E * SLOTS).rearrange("p (c e s) -> p c e s", c=2, e=E)
        hidden = carve(RING * SLOTS).rearrange("p (r s) -> p r s", r=RING)
        silu_g = carve(2 * SLOTS).rearrange("p (r s) -> p r s", r=2)
        y_out = carve(2 * C).rearrange("p (r c) -> p r c", r=2)
        place = sb("place", [TT, E])
        over_place = sb("over_place", [TT])
        counts = ctx.enter_context(nc.sbuf_tensor("counts", [1, E + 1], mybir.dt.int32))
        acc = sb("acc", [TT, C])
        logit = sb("logit", [TT, E])
        ex = sb("ex", [TT, E])
        gate = sb("gate", [TT, E])
        pick = sb("pick", [4, TT, E])
        tmp = sb("tmp", [TT, E])
        red = sb("red", [8, TT])
        combT = oT[:, 0, :]

        bank = [ctx.enter_context(nc.psum_tensor(f"bank{i}", [P, BANK], F32)) for i in range(8)]

        x_landed, const_landed, par_landed, rel_landed = (sem(s) for s in ("x_landed", "const_landed", "par_landed", "rel_landed"))
        att_landed = [sem(f"att_landed{i}") for i in range(2)]
        e0_landed = [sem(f"e0_landed{i}") for i in range(E)]
        e1_landed = [sem(f"e1_landed{i}") for i in range(E)]
        bias_landed = sem("bias_landed")
        ones_set = sem("ones_set")
        vec_step, pool_step, act_step = sem("vec_step"), sem("pool_step"), sem("act_step")
        stats_ready, rstd_ready, xn_ready = sem("stats_ready"), sem("rstd_ready"), sem("xn_ready")
        xnT_psum, xnT_act, xnT_vec = sem("xnT_psum"), sem("xnT_act"), sem("xnT_vec")
        q_psum, k_psum, v_psum, rel_psum = sem("q_psum"), sem("k_psum"), sem("v_psum"), sem("rel_psum")
        q_ready, q_rounded, q_split = sem("q_ready"), sem("q_rounded"), sem("q_split")
        k_ready, k_rounded, k_split, v_ready = sem("k_ready"), sem("k_rounded"), sem("k_split"), sem("v_ready")
        rel_half, rel_ready, rel_rounded, rel_split = sem("rel_half"), sem("rel_ready"), sem("rel_rounded"), sem("rel_split")
        scores_psum, max_ready, probs_ready = sem("scores_psum"), sem("max_ready"), sem("probs_ready")
        probsT_psum, probsT_vec, probsT_act = sem("probsT_psum"), sem("probsT_vec"), sem("probsT_act")
        o_copied, o_turned = sem("o_copied"), sem("o_turned")
        o_psum, o_ready, oT_psum, oT_ready = sem("o_psum"), sem("o_ready"), sem("oT_psum"), sem("oT_ready")
        proj_psum, x_ready = sem("proj_psum"), sem("x_ready")
        logit_psum, logit_ready, exp_ready = sem("logit_psum"), sem("logit_ready"), sem("exp_ready")
        gate_ready = sem("gate_ready")
        combT_psum, combT_ready, bias2_psum = sem("combT_psum"), sem("combT_ready"), sem("bias2_psum")
        acc_ready = sem("acc_ready")
        xn_rounded, xn_split = sem("xn_rounded"), sem("xn_split")
        picked, place_psum, place_ready, counts_ready = sem("picked"), sem("place_psum"), sem("place_ready"), sem("counts_ready")
        chosen_ready, weighted_ready = sem("chosen_ready"), sem("weighted_ready")
        xe_psum, xe_act, xe_vec = sem("xe_psum"), sem("xe_act"), sem("xe_vec")
        weightedT_psum, weightedT_act, weightedT_vec = sem("weightedT_psum"), sem("weightedT_act"), sem("weightedT_vec")
        moe_done = sem("moe_done")

        def stream_sems(name):
            return {s: sem(f"{s}_{name}") for s in
                    ("up_psum", "silu_ready", "hidden_vec", "hidden_act", "hidden_used", "y_ready", "combined")}

        main = [stream_sems(f"main{layer}") for layer in range(2)]
        over = [[None] + [stream_sems(f"over{layer}_{i}") for i in range(1, PASSES)] for layer in range(2)]
        over_chosen, over_gathered, over_x = (
            [[None] + [sem(f"{s}{layer}_{i}") for i in range(1, PASSES)] for layer in range(2)]
            for s in ("over_chosen", "over_gathered", "over_x"))
        out_landed = sem("out_landed")

        tiles0 = [(e, t, min(P, HID0[e] - t * P)) for e in range(E) for t in range(TILES0[e])]
        tiles1 = [(e, t, P) for e in range(E) for t in range(TILES1)]
        tiles = (tiles0, tiles1)
        first_tile = [[next(n for n, tile in enumerate(ts) if tile[0] == e) for e in range(E)] + [len(ts)] for ts in tiles]

        def hidden_by_act(layer, n):
            return layer == 1 and n % 2 == 1

        def hidden_counts(layer, n):
            act = sum(hidden_by_act(layer, i) for i in range(n))
            return n - act, act

        def wait_hidden(eng, layer, sems, n):
            vec, act = hidden_counts(layer, n + 1)
            if hidden_by_act(layer, n):
                eng.wait_ge(sems["hidden_act"], act)
            else:
                eng.wait_ge(sems["hidden_vec"], vec)

        def up_bank(layer, n, part=0):
            return bank[2 * (n % 2) + part] if layer == 0 else bank[n % 4]

        LAST_PAIR_AT = (2, 0)

        OVER_CHOSEN = 1 + 2 * TT

        def weightedT_bank(pair):
            return bank[(5, 6, 7, 7)[pair]]

        def y_bank(e):
            return bank[5 + e % 2]

        def extra_passes(eng, layer, body, skipped):
            eng.wait_ge(counts_ready, layer + 1)
            most = eng.value_load(counts[0:1, E:E + 1], min_val=0, max_val=TOK)
            for i in range(1, PASSES):
                with eng.If(most > i * SLOTS):
                    for e in range(E):
                        n = eng.value_load(counts[0:1, e:e + 1], min_val=0, max_val=TOK)
                        with eng.If(n > i * SLOTS):
                            body(i, e)
                        with eng.Else():
                            for s, k in skipped(i, e):
                                if k:
                                    eng.drain().then_inc(s, k)

        def tiles_of(layer, e):
            return range(first_tile[layer][e], first_tile[layer][e + 1])

        def turned_by_act(n):
            return n % 3 == 2

        def wait_probsT(eng, n):
            if turned_by_act(n):
                eng.wait_ge(probsT_act, (n + 1) // 3)
            else:
                eng.wait_ge(probsT_vec, n + 1 - (n + 1) // 3)

        block = ctx.enter_context(nc.Block())

        @block.sync
        def _(sp):
            sp.dma_start(x[:], x_in.rearrange("(t p) c -> p t c", p=P)).then_inc(x_landed, 16)
            sp.dma_start(const[:], const_in[:, 0:CONST_W]).then_inc(const_landed, 16)
            sp.dma_start(att_hi[:], weights_hi[0]).then_inc(att_landed[0], 16)
            sp.dma_start(att_lo[0:CL, :], weights_lo[0]).then_inc(att_landed[0], 16)
            sp.dma_start(par[:], params).then_inc(par_landed, 16)
            sp.dma_start(rel_t[:], rel_in).then_inc(rel_landed, 16)
            sp.dma_start(onehot[:], const_in[:, CONST_W:CONST_W + TOK]).then_inc(rel_landed, 16)
            sp.dma_start(bias1[:], bias1_in).then_inc(bias_landed, 16)
            sp.dma_start(bias2[0:E, :], bias2_in).then_inc(bias_landed, 16)
            for e in range(E):
                sp.dma_start(w0[:, OFF0[e]:OFF0[e + 1]], experts0[:, OFF0[e]:OFF0[e + 1]]).then_inc(e0_landed[e], 16)
            sp.wait_ge(logit_psum, 1)
            sp.dma_start(att_hi[:], weights_hi[1]).then_inc(att_landed[1], 16)
            sp.dma_start(att_lo[0:CL, :], weights_lo[1]).then_inc(att_landed[1], 16)
            sp.wait_ge(moe_done, 1)
            for e in range(E):
                sp.dma_start(w0[:, e * SIZE1:(e + 1) * SIZE1], experts1[:, e]).then_inc(e1_landed[e], 16)
            sp.wait_ge(x_ready, 4)
            sp.dma_start(out.rearrange("(t p) c -> p t c", p=P), x[:]).then_inc(out_landed, 16)
            sp.wait_ge(out_landed, 16)

        @block.gpsimd
        def _(pool):
            nc.gpsimd.memset(v1[:, :, :, HD:HD + 1], 1.0).then_inc(ones_set, 1)
            nc.gpsimd.memset(v1[:, :, :, HD + 1:SLOT], 0.0).then_inc(ones_set, 1)
            nc.gpsimd.memset(ones[:], 1.0).then_inc(ones_set, 1)
            pool.wait_ge(const_landed, 16)
            pool.wait_ge(rel_landed, 32)
            nc.gpsimd.tensor_copy(onehot_r[:], onehot[:]).then_inc(ones_set, 1)
            for n in range(4):
                pool.wait_ge(stats_ready, n + 1)
                nc.gpsimd.tensor_scalar(var_eps[:], mean_var[:, :, 1], LN_EPS[n], None, ALU.add).then_inc(pool_step, 1)
                pool.wait_ge(pool_step, n + 1)
                nc.gpsimd.tensor_tensor(rstd[:], var_eps[:], small[:, 0:1].to_broadcast([P, TT]), ALU.pow).then_inc(rstd_ready, 1)
                if n % 2 == 0:
                    layer = n // 2
                    for g in range(HG):
                        pool.wait_ge(k_ready, HG * layer + g + 1)
                        pool.wait_ge(k_rounded, HG * layer + g + 1)
                        nc.gpsimd.tensor_tensor(k_lo[:, g], kT[:, g], k_hi[:, g].bitcast(F32), ALU.subtract).then_inc(k_split, 1)
                    if layer == 0:
                        pool.wait_ge(rel_ready, 2 * HG)
                        for g in range(HG):
                            pool.wait_ge(rel_rounded, g + 1)
                            nc.gpsimd.tensor_tensor(rel_lo[:, g], relT[:, g], rel_hi[:, g].bitcast(F32), ALU.subtract).then_inc(rel_split, 1)
                else:
                    layer = n // 2
                    pool.wait_ge(xn_ready, 2 * TT * (n + 1))
                    pool.wait_ge(xn_rounded, layer + 1)
                    nc.gpsimd.tensor_tensor(xn_lo, xn[:], xn_hi.bitcast(F32), ALU.subtract).then_inc(xn_split, 1)
                    if layer == 0:
                        nc.gpsimd.tensor_tensor(acc[:], x[:], xn[:, :, 0:C], ALU.add).then_inc(acc_ready, 1)
                    pool.wait_ge(place_ready, layer + 1)
                    pool.wait_ge(gate_ready, layer + 1)
                    pool.wait_ge(probsT_psum, (layer + 1) * HEADS)
                    for e in range(E):
                        for t in range(TT):
                            nc.gpsimd.tensor_scalar(weighted[:, t, e, :], places, place[:, t, e:e + 1], gate[:, t, e:e + 1],
                                                    ALU.is_equal, ALU.mult).then_inc(weighted_ready, 1)

        @block.scalar
        def _(act):
            def norm_T(n):
                act.wait_ge(xnT_psum, n + 1)
                nc.scalar.copy(xnT[:, 0, :], bank[6][:, 0:TOK]).then_inc(xnT_act, 1)

            def copy_o(layer, g):
                act.wait_ge(o_psum, layer * HEADS + (g + 1) * HB)
                act.wait_ge(q_split, HG * (layer + 1))
                nc.scalar.copy(qT[:, g, :], bank[6 + g % 2][:, 0:TOK]).then_inc(o_copied, 1)

            def copy_weightedT(layer, pair):
                act.wait_ge(weightedT_psum, 4 * layer + pair + 1)
                nc.scalar.copy(weightedT[0:SLOTS, 2 * pair:2 * pair + 2].rearrange("p e t -> p (e t)"),
                               weightedT_bank(pair)[0:SLOTS, :]).then_inc(weightedT_act, 1)

            def stream(layer, sems, ns, main_layer=None):
                for n in ns:
                    e, t, m = tiles[layer][n]
                    if layer == 0:
                        act.wait_ge(sems["up_psum"], n + 1)
                        if n >= 2:
                            wait_hidden(act, 0, sems, n - 2)
                        nc.scalar.activation(silu_g[0:m, n % 2, :], up_bank(0, n)[0:m, 0:SLOTS], ACT.Silu).then_inc(sems["silu_ready"], 1)
                    elif hidden_by_act(layer, n):
                        act.wait_ge(sems["up_psum"], n + 1)
                        if n >= RING:
                            act.wait_ge(sems["hidden_used"], n - RING + 1)
                        nc.scalar.activation(hidden[:, n % RING, :], up_bank(1, n)[:, 0:SLOTS], ACT.Relu,
                                             bias=bias1[:, e * TILES1 + t:e * TILES1 + t + 1]).then_inc(sems["hidden_act"], 1)
                    if main_layer is not None and (e, t) == LAST_PAIR_AT:
                        copy_weightedT(layer, 3)

            def over_counts(layer, i, e):
                k = first_tile[layer][e + 1] - first_tile[layer][e]
                if layer == 0:
                    return [(over[0][i]["silu_ready"], k)]
                return [(over[1][i]["hidden_act"], hidden_counts(1, first_tile[1][e + 1])[1] - hidden_counts(1, first_tile[1][e])[1])]

            act.wait_ge(par_landed, 16)
            for layer in range(2):
                norm_T(2 * layer)
                act.wait_ge(q_psum, layer + 1)
                for g in range(HG):
                    for part, done in ((q_round, q_rounded), (qT, q_ready)):
                        nc.scalar.activation(part[:, g, :], bank[g // 2][:, (g % 2) * TOK:(g % 2 + 1) * TOK], ACT.Identity,
                                             bias=par[:, layer, B_QK + g:B_QK + g + 1]).then_inc(done, 1)
                if layer == 0:
                    act.wait_ge(rel_psum, 1)
                    for half in range(2):
                        rows = relT[:].rearrange("p g (r c) -> p r g c", c=GRID)[:, 8 * half:8 * half + 8]
                        nc.scalar.activation(rows, bank[5 + half][:, 0:HG * P].rearrange("p (r g c) -> p r g c", r=8, g=HG),
                                             ACT.Copy, scale=small[:, 1:2]).then_inc(rel_half, 1)
                for h in range(HEADS + 2):
                    if h < HEADS:
                        head = layer * HEADS + h
                        act.wait_ge(max_ready, head + 1)
                        if head >= HB:
                            act.wait_ge(probsT_psum, head - HB + 1)
                        if h == 0 and layer == 1:
                            act.wait_ge(moe_done, 1)
                        for t in range(TT):
                            nc.scalar.activation(probs[:, h % HB, t, :], bank[h % HB][:, t * TOK:(t + 1) * TOK], ACT.Exp,
                                                 bias=neg_max[:, h, t:t + 1]).then_inc(probs_ready, 1)
                    if h >= 2 and turned_by_act(layer * HEADS + h - 2):
                        head = layer * HEADS + h - 2
                        act.wait_ge(probsT_psum, head + 1)
                        if head >= TRING:
                            act.wait_ge(o_psum, head - TRING + 1)
                        nc.scalar.copy(probsT[:, head % TRING], bank[4 + head % 2][:]).then_inc(probsT_act, 1)
                    if h >= HB + 3 and (h - 3) % HB == 0:
                        copy_o(layer, (h - 3) // HB - 1)
                copy_o(layer, HG - 1)
                act.wait_ge(oT_psum, layer + 1)
                nc.scalar.copy(oT[:, 0, :], bank[7][:, 0:TOK]).then_inc(oT_ready, 1)
                nc.scalar.copy(oT[0:CL, 1, :], bank[7][0:CL, TOK:2 * TOK]).then_inc(oT_ready, 1)
                norm_T(2 * layer + 1)
                act.wait_ge(logit_ready, layer + 1)
                nc.scalar.activation(ex[:], logit[:], ACT.Exp).then_inc(exp_ready, 1)
                act.wait_ge(o_psum, (layer + 1) * HEADS)
                for batch in range(2):
                    act.wait_ge(xe_psum, 4 * layer + 2 * batch + 1)
                    nc.scalar.copy(xe[:, 0, 4 * batch:4 * batch + 4].rearrange("p e s -> p (e s)"), bank[2 * batch][:, 0:4 * SLOTS]).then_inc(xe_act, 1)
                copy_weightedT(layer, 1)
                if layer == 1:
                    act.wait_ge(bias_landed, 32)
                stream(layer, main[layer], range(len(tiles[layer])), layer)
                extra_passes(act, layer, lambda i, e: stream(layer, over[layer][i], tiles_of(layer, e)),
                             lambda i, e: over_counts(layer, i, e))

        @block.vector
        def _(dve):
            steps = [0]

            def step(ins):
                steps[0] += 1
                ins.then_inc(vec_step, 1)
                dve.wait_ge(vec_step, steps[0])

            def norm(n):
                for t in range(TT):
                    step(nc.vector.bn_stats(stats[:, t, :], x[:, t, :]))
                step(nc.vector.bn_aggr(mean_var[:, 0, :], stats[:, 0, :]))
                nc.vector.bn_aggr(mean_var[:, 1, :], stats[:, 1, :]).then_inc(stats_ready, 1)
                dve.wait_ge(rstd_ready, n + 1)
                for t in range(TT):
                    nc.vector.tensor_scalar(xn[:, t, 0:C], x[:, t, :], mean_var[:, t, 0:1], rstd[:, t:t + 1],
                                            ALU.subtract, ALU.mult).then_inc(xn_ready, 1)
                    nc.vector.tensor_scalar(xn[:, t, C:C + CL], x[:, t, P:C], mean_var[:, t, 0:1], rstd[:, t:t + 1],
                                            ALU.subtract, ALU.mult).then_inc(xn_ready, 1)
                dve.wait_ge(xnT_psum, n + 1)
                nc.vector.tensor_copy(xnT[:, 1, :], bank[7][:, 0:TOK]).then_inc(xnT_vec, 1)

            def attend(layer):
                dve.wait_ge(k_psum, layer + 1)
                if layer == 1:
                    dve.wait_ge(scores_psum, HEADS)
                for g in range(HG):
                    for part, done in ((k_hi, k_rounded), (kT, k_ready)):
                        nc.vector.tensor_scalar(part[:, g, :], bank[2 + g // 2][:, (g % 2) * TOK:(g % 2 + 1) * TOK],
                                                par[:, layer, B_QK + HG + g:B_QK + HG + g + 1], SCALE,
                                                ALU.add, ALU.mult).then_inc(done, 1)
                    dve.wait_ge(q_ready, HG * layer + g + 1)
                    dve.wait_ge(q_rounded, HG * layer + g + 1)
                    nc.vector.scalar_tensor_tensor(q_parts[:, g], q_round[:, g].bitcast(F32), small[:, 3:4], qT[:, g],
                                                   ALU.mult, ALU.add).then_inc(q_split, 1)
                dve.wait_ge(v_psum, layer + 1)
                for t in range(TT):
                    nc.vector.tensor_tensor(v1[:, t, :, 0:HD], bank[4][:, t * C:(t + 1) * C].rearrange("p (h d) -> p h d", d=HD),
                                            par[:, layer, B_V:B_V + C].rearrange("p (h d) -> p h d", d=HD), ALU.add).then_inc(v_ready, 1)
                if layer == 0:
                    dve.wait_ge(rel_psum, 2)
                    dve.wait_ge(rel_half, 2)
                    for half, b in enumerate((7, 0)):
                        for g in range(HG):
                            cols = relT[:, g, :].rearrange("p (r c) -> p c r", c=GRID)[:, 8 * half:8 * half + 8]
                            new = bank[b][:, 0:HG * P].rearrange("p (c g r) -> p c g r", c=8, g=HG)[:, :, g]
                            nc.vector.scalar_tensor_tensor(cols, new, small[:, 2:3], cols, ALU.mult, ALU.add).then_inc(rel_ready, 1)
                    dve.wait_ge(rel_ready, 2 * HG)
                    for g in range(HG):
                        nc.vector.tensor_copy(rel_hi[:, g], relT[:, g]).then_inc(rel_rounded, 1)
                for h in range(HEADS + 2):
                    if h < HEADS:
                        dve.wait_ge(scores_psum, layer * HEADS + h + 1)
                        nc.vector.tensor_reduce(neg_max[:, h, :], bank[h % HB][:].rearrange("p (t k) -> p t k", t=TT),
                                                AX_X, ALU.max, negate=True).then_inc(max_ready, 1)
                    if h >= 2 and not turned_by_act(layer * HEADS + h - 2):
                        head = layer * HEADS + h - 2
                        dve.wait_ge(probsT_psum, head + 1)
                        if head >= TRING:
                            dve.wait_ge(o_psum, head - TRING + 1)
                        nc.vector.tensor_copy(probsT[:, head % TRING], bank[4 + head % 2][:]).then_inc(probsT_vec, 1)
                dve.wait_ge(o_turned, layer + 1)
                for t in range(TT):
                    o = bank[t][:, 0:QK].rearrange("p (h d) -> p h d", d=SLOT)
                    step(nc.vector.reciprocal(o_sum[:, t, :], o[:, :, HD]))
                    nc.vector.tensor_tensor(o_tok[:, t, :].rearrange("p (h d) -> p h d", d=HD), o[:, :, 0:HD],
                                            o_sum[:, t, :].unsqueeze(2).to_broadcast([P, HEADS, HD]), ALU.mult).then_inc(o_ready, 1)
                    step(nc.vector.tensor_tensor(x[:, t, :], x[:, t, :], par[:, layer, B_O:B_O + C], ALU.add))
                dve.wait_ge(proj_psum, layer + 1)
                for t in range(TT):
                    step(nc.vector.tensor_tensor(x[:, t, :], x[:, t, :], bank[4][:, t * C:(t + 1) * C], ALU.add))

            def round_xn(layer):
                dve.wait_ge(xn_ready, 2 * TT * (2 * layer + 2))
                dve.wait_ge(scores_psum, (layer + 1) * HEADS)
                nc.vector.tensor_copy(xn_hi, xn[:]).then_inc(xn_rounded, 1)

            def bc(a):
                return a.unsqueeze(2).to_broadcast([P, TT, E])

            def route(layer):
                dve.wait_ge(logit_psum, layer + 1)
                lp = bank[5][:, 0:TT * E].rearrange("p (t e) -> p t e", e=E)
                if layer == 0:
                    step(nc.vector.tensor_copy(logit[:], lp))
                else:
                    for t in range(TT):
                        step(nc.vector.tensor_tensor(logit[:, t], lp[:, t], par[:, 1, B_GATE:B_GATE + E], ALU.add))
                step(nc.vector.tensor_reduce(red[:, 0], logit[:], AX_X, ALU.max))
                nc.vector.tensor_tensor(logit[:], logit[:], bc(red[:, 0]), ALU.subtract).then_inc(logit_ready, 1)
                dve.wait_ge(exp_ready, layer + 1)
                step(nc.vector.tensor_reduce(red[:, 1], ex[:], AX_X, ALU.add))
                step(nc.vector.reciprocal(red[:, 2], red[:, 1]))
                step(nc.vector.tensor_tensor(gate[:], ex[:], bc(red[:, 2]), ALU.mult))
                rank = small[:, 4:4 + E].unsqueeze(1).to_broadcast([P, TT, E])
                step(nc.vector.tensor_copy(tmp[:], gate[:]))
                for k in range(2):
                    step(nc.vector.tensor_reduce(red[:, 3], tmp[:], AX_X, ALU.max))
                    step(nc.vector.tensor_tensor(pick[:, 2], tmp[:], bc(red[:, 3]), ALU.is_equal))
                    step(nc.vector.tensor_tensor(pick[:, 2], pick[:, 2], rank, ALU.mult))
                    step(nc.vector.tensor_reduce(red[:, 4], pick[:, 2], AX_X, ALU.max))
                    step(nc.vector.tensor_tensor(pick[:, k], pick[:, 2], bc(red[:, 4]), ALU.is_equal))
                    if k == 0:
                        step(nc.vector.scalar_tensor_tensor(tmp[:], pick[:, 0], -2.0, tmp[:], ALU.mult, ALU.add))
                nc.vector.tensor_tensor(pick[:, 3], pick[:, 0], pick[:, 1], ALU.add).then_inc(picked, 1)
                dve.wait_ge(picked, layer + 1)
                last = nc.vector.tensor_tensor(gate[:], gate[:], pick[:, 3], ALU.mult)
                if layer == 1:
                    step(last)
                    step(nc.vector.tensor_reduce(red[:, 5], gate[:], AX_X, ALU.add))
                    step(nc.vector.reciprocal(red[:, 6], red[:, 5]))
                    last = nc.vector.tensor_tensor(gate[:], gate[:], bc(red[:, 6]), ALU.mult)
                last.then_inc(gate_ready, 1)
                dve.wait_ge(place_psum, layer + 1)
                nc.vector.scalar_tensor_tensor(place[:], bank[4][:, 0:TT * E].rearrange("p (t e) -> p t e", e=E), 1.0, pick[:, 3],
                                               ALU.add, ALU.mult).then_inc(place_ready, 1)
                dve.wait_ge(place_ready, layer + 1)

            def copy_weightedT(layer, pair):
                dve.wait_ge(weightedT_psum, 4 * layer + pair + 1)
                nc.vector.tensor_copy(weightedT[0:SLOTS, 2 * pair:2 * pair + 2].rearrange("p e t -> p (e t)"),
                                      weightedT_bank(pair)[0:SLOTS, :]).then_inc(weightedT_vec, 1)

            def copy_y(sems, e):
                if e >= 2:
                    dve.wait_ge(sems["combined"], e - 1)
                nc.vector.tensor_copy(y_out[0:SLOTS, e % 2, :], y_bank(e)[0:SLOTS, 0:C]).then_inc(sems["y_ready"], 1)

            def stream(layer, sems, ns, end):
                for n in ns:
                    e, t, m = tiles[layer][n]
                    if layer == 0:
                        dve.wait_ge(sems["silu_ready"], n + 1)
                        if n >= RING:
                            dve.wait_ge(sems["hidden_used"], n - RING + 1)
                        nc.vector.tensor_tensor(hidden[0:m, n % RING, :], silu_g[0:m, n % 2, :], up_bank(0, n, 1)[0:m, 0:SLOTS],
                                                ALU.mult).then_inc(sems["hidden_vec"], 1)
                    elif not hidden_by_act(layer, n):
                        dve.wait_ge(sems["up_psum"], n + 1)
                        if n >= RING:
                            dve.wait_ge(sems["hidden_used"], n - RING + 1)
                        nc.vector.tensor_scalar(hidden[:, n % RING, :], up_bank(1, n)[:, 0:SLOTS],
                                                bias1[:, e * TILES1 + t:e * TILES1 + t + 1], 0.0, ALU.add, ALU.max).then_inc(sems["hidden_vec"], 1)
                    if t == LAG and n - t - 1 in ns:
                        dve.wait_ge(sems["hidden_used"], n - t)
                        copy_y(sems, e - 1)
                    if end == "main" and (e, t) == (1, 0):
                        copy_weightedT(layer, 2)
                e = tiles[layer][ns[-1]][0]
                dve.wait_ge(sems["hidden_used"], ns[-1] + 1)
                copy_y(sems, e)

            def extra(layer, i, e):
                done = over_chosen[layer][i]
                nc.vector.tensor_scalar(over_place[:], place[:, :, e], -float(i * SLOTS), None, ALU.add).then_inc(done, 1)
                dve.wait_ge(done, OVER_CHOSEN * e + 1)
                for t in range(TT):
                    nc.vector.tensor_scalar(chosen[:, t, 0, :], places, over_place[:, t:t + 1], None, ALU.is_equal).then_inc(done, 1)
                    nc.vector.tensor_scalar(weighted[:, t, 0, :], places, over_place[:, t:t + 1], gate[:, t, e:e + 1],
                                            ALU.is_equal, ALU.mult).then_inc(done, 1)
                dve.wait_ge(over_gathered[layer][i], e + 1)
                for c in range(2):
                    nc.vector.tensor_copy(xe[:, c, 0, :], bank[c][:, 0:SLOTS]).then_inc(over_x[layer][i], 1)
                nc.vector.tensor_copy(weightedT[0:SLOTS, 0, :], bank[7][0:SLOTS, 0:TOK]).then_inc(over_x[layer][i], 1)
                stream(layer, over[layer][i], tiles_of(layer, e), "over")
                dve.wait_ge(over[layer][i]["combined"], e + 1)

            def experts(layer):
                dve.wait_ge(scores_psum, (layer + 1) * HEADS)
                for e in range(E):
                    for t in range(TT):
                        nc.vector.tensor_scalar(chosen[:, t, e, :], places, place[:, t, e:e + 1], None, ALU.is_equal).then_inc(chosen_ready, 1)
                step(nc.vector.tensor_copy(counts[0:1, 0:E], bank[4][0:1, TT * E:(TT + 1) * E]))
                nc.vector.tensor_reduce(counts[0:1, E:E + 1], bank[4][0:1, TT * E:(TT + 1) * E], AX_X, ALU.max).then_inc(counts_ready, 1)
                if layer == 1:
                    dve.wait_ge(combT_psum, 1)
                    nc.vector.tensor_copy(combT[0:E, :], bank[5][0:E, P:P + TOK]).then_inc(combT_ready, 1)
                    dve.wait_ge(bias_landed, 32)
                for batch in range(2):
                    dve.wait_ge(xe_psum, 4 * layer + 2 * batch + 2)
                    nc.vector.tensor_copy(xe[:, 1, 4 * batch:4 * batch + 4].rearrange("p e s -> p (e s)"), bank[2 * batch + 1][:, 0:4 * SLOTS]).then_inc(xe_vec, 1)
                copy_weightedT(layer, 0)
                stream(layer, main[layer], range(len(tiles[layer])), "main")
                dve.wait_ge(main[layer]["combined"], E)

                def skipped(i, e):
                    vec = hidden_counts(layer, first_tile[layer][e + 1])[0] - hidden_counts(layer, first_tile[layer][e])[0]
                    return [(over_chosen[layer][i], OVER_CHOSEN), (over_x[layer][i], 3), (over[layer][i]["hidden_vec"], vec), (over[layer][i]["y_ready"], 1)]

                extra_passes(dve, layer, lambda i, e: extra(layer, i, e), skipped)

            dve.wait_ge(x_landed, 16)
            dve.wait_ge(par_landed, 16)
            norm(0)
            dve.wait_ge(const_landed, 16)
            attend(0)
            norm(1)
            round_xn(0)
            route(0)
            experts(0)
            dve.wait_ge(acc_ready, 1)
            nc.vector.tensor_tensor(x[:], acc[:], bank[4][:, 0:TT * C].rearrange("p (t c) -> p t c", t=TT), ALU.add).then_inc(moe_done, 1)
            dve.wait_ge(moe_done, 1)
            norm(2)
            attend(1)
            norm(3)
            round_xn(1)
            route(1)
            experts(1)
            for t in range(TT):
                nc.vector.tensor_tensor(x[:, t, :], x[:, t, :], bank[4][:, t * C:(t + 1) * C], ALU.add).then_inc(x_ready, 2)

        @block.tensor
        def _(pe):
            def norm_T(n):
                pe.wait_ge(xn_ready, 2 * TT * (n + 1))
                if n == 2:
                    pe.wait_ge(moe_done, 1)
                for t in range(TT):
                    cols = slice(t * P, (t + 1) * P)
                    nc.tensor.transpose(bank[6][:, cols], xn[:, t, 0:P], ident)
                    last = nc.tensor.transpose(bank[7][:, cols], xn[:, t, P:C + CL], ident)
                last.then_inc(xnT_psum, 1)
                pe.wait_ge(xnT_act, n + 1)
                pe.wait_ge(xnT_vec, n + 1)

            def project(out_ap, cols):
                nc.tensor.matmul(out_ap, att_hi[:, cols], xnT[:, 0, :], start=True, stop=False)
                return nc.tensor.matmul(out_ap, att_lo[0:CL, cols], xnT[0:CL, 1, :], start=False, stop=True)

            def project_tokens(out_ap, t, cols):
                tok = slice(t * P, (t + 1) * P)
                nc.tensor.matmul(out_ap, xnT[:, 0, tok], att_hi[:, cols], start=True, stop=False)
                return nc.tensor.matmul(out_ap, xnT[0:CL, 1, tok], att_lo[0:CL, cols], start=False, stop=True)

            def scores(layer, pair):
                heads = (2 * pair, 2 * pair + 1)
                g = heads[0] // HB
                pe.wait_ge(q_split, HG * layer + g + 1)
                pe.wait_ge(k_rounded, HG * layer + g + 1)
                pe.wait_ge(k_split, HG * layer + g + 1)
                if layer == 0:
                    pe.wait_ge(rel_split, g + 1)
                for h in heads:
                    if layer * HEADS + h >= HB:
                        pe.wait_ge(probs_ready, TT * (layer * HEADS + h - HB + 1))
                terms = [(q_parts, k_hi), (q_parts, k_lo)]
                if layer == 0:
                    terms += [(rel_hi, None), (rel_lo, None)]
                for t in range(TT):
                    for i, (left, right) in enumerate(terms):
                        for h in heads:
                            b = h % HB
                            rows = slice(SLOT * b, SLOT * (b + 1))
                            last = nc.tensor.matmul(bank[b][:, t * TOK:(t + 1) * TOK], left[rows, g, t * P:(t + 1) * P],
                                                    right[rows, g, :] if right is not None else onehot_r[rows, :],
                                                    start=i == 0, stop=i == len(terms) - 1, tile_position=(SLOT * b, 0))
                            if t == TT - 1 and i == len(terms) - 1:
                                last.then_inc(scores_psum, 1)

            def turn(layer, h):
                head = layer * HEADS + h
                pe.wait_ge(probs_ready, TT * (head + 1))
                if head >= 2:
                    wait_probsT(pe, head - 2)
                for k in range(TT):
                    for t in range(TT):
                        at = k * TOK + t * P
                        last = nc.tensor.transpose(bank[4 + head % 2][:, at:at + P], probs[:, h % HB, t, k * P:(k + 1) * P], ident)
                last.then_inc(probsT_psum, 1)

            def weigh(layer, h):
                head = layer * HEADS + h
                wait_probsT(pe, head)
                g, b = h // HB, h % HB
                if b == 0 and g >= 2:
                    pe.wait_ge(o_copied, HG * layer + g - 1)
                for k in range(TT):
                    last = nc.tensor.matmul(bank[6 + g % 2][SLOT * b:SLOT * (b + 1), 0:TOK], v1[:, k, h, :],
                                            probsT[:, head % TRING, k, :], start=k == 0, stop=k == TT - 1,
                                            tile_position=(0, SLOT * b))
                last.then_inc(o_psum, 1)

            def attend(layer):
                pe.wait_ge(att_landed[layer], 32)
                for g in range(HG):
                    last = project(bank[g // 2][:, (g % 2) * TOK:(g % 2 + 1) * TOK], slice(W_QK + g * P, W_QK + (g + 1) * P))
                last.then_inc(q_psum, 1)
                for g in range(HG):
                    last = project(bank[2 + g // 2][:, (g % 2) * TOK:(g % 2 + 1) * TOK],
                                   slice(W_QK + QK + g * P, W_QK + QK + (g + 1) * P))
                last.then_inc(k_psum, 1)
                for t in range(TT):
                    last = project_tokens(bank[4][:, t * C:(t + 1) * C], t, slice(W_V, W_V + C))
                last.then_inc(v_psum, 1)
                pe.wait_ge(q_ready, HG * (layer + 1))
                if layer == 0:
                    pe.wait_ge(rel_landed, 32)
                    for axis, banks in enumerate(((5, 6), (7, 0))):
                        order = "p g (r c) -> p r g c" if axis == 0 else "p g (r c) -> p c g r"
                        lines = qT[:].rearrange(order, c=GRID)
                        for i in range(GRID):
                            window = rel_t[:, axis, GRID - 1 - i:GRID - 1 - i + P]
                            at = (i % 8) * HG * GRID
                            last = nc.tensor.matmul(bank[banks[i // 8]][:, at:at + HG * GRID], window, lines[:, i],
                                                    start=True, stop=True)
                        last.then_inc(rel_psum, 1)
                    pe.wait_ge(rel_ready, 2 * HG)
                pe.wait_ge(k_ready, HG * (layer + 1))
                pe.wait_ge(v_ready, TT * (layer + 1))
                pe.wait_ge(ones_set, 4)
                scores(layer, 0)
                for h in range(HEADS):
                    if h % 2 == 0 and h + 2 < HEADS:
                        scores(layer, h // 2 + 1)
                    turn(layer, h)
                    if h >= 2:
                        weigh(layer, h - 2)
                weigh(layer, HEADS - 2)
                weigh(layer, HEADS - 1)
                pe.wait_ge(o_copied, HG * (layer + 1))
                for t in range(TT):
                    for g in range(HG):
                        last = nc.tensor.transpose(bank[t][:, g * P:(g + 1) * P], qT[:, g, t * P:(t + 1) * P], ident)
                last.then_inc(o_turned, 1)
                pe.wait_ge(o_ready, TT * (layer + 1))
                for t in range(TT):
                    nc.tensor.transpose(bank[7][:, t * P:(t + 1) * P], o_tok[:, t, 0:P], ident)
                    last = nc.tensor.transpose(bank[7][0:CL, TOK + t * P:TOK + (t + 1) * P], o_tok[:, t, P:C], ident)
                last.then_inc(oT_psum, 1)
                pe.wait_ge(oT_ready, 2 * (layer + 1))
                for t in range(TT):
                    tok = slice(t * P, (t + 1) * P)
                    nc.tensor.matmul(bank[4][:, t * C:(t + 1) * C], oT[:, 0, tok], att_hi[:, W_OUT:W_OUT + C], start=True, stop=False)
                    last = nc.tensor.matmul(bank[4][:, t * C:(t + 1) * C], oT[0:CL, 1, tok], att_lo[0:CL, W_OUT:W_OUT + C],
                                            start=False, stop=True)
                last.then_inc(proj_psum, 1)

            def router(layer):
                for t in range(TT):
                    last = project_tokens(bank[5][:, t * E:(t + 1) * E], t, slice(W_ROUTER, W_ROUTER + E))
                last.then_inc(logit_psum, 1)

            def places_of(layer):
                pe.wait_ge(picked, layer + 1)
                pe.wait_ge(ones_set, 4)
                mask = pick[:, 3]
                nc.tensor.matmul(bank[4][:, 0:E], upper, mask[:, 0], start=True, stop=True)
                nc.tensor.matmul(bank[4][:, E:2 * E], ones[:], mask[:, 0], start=True, stop=False)
                nc.tensor.matmul(bank[4][:, E:2 * E], upper, mask[:, 1], start=False, stop=True)
                for t in range(TT):
                    last = nc.tensor.matmul(bank[4][:, 2 * E:3 * E], ones[:], mask[:, t], start=t == 0, stop=t == TT - 1)
                last.then_inc(place_psum, 1)

            def gather(out_ap, c, tokens):
                for i, part in enumerate((xn_hi, xn_lo)):
                    for t in range(TT):
                        last = nc.tensor.matmul(out_ap, part[:, t, c * P:(c + 1) * P], tokens(t),
                                                start=i == 0 and t == 0, stop=i == 1 and t == TT - 1)
                return last

            def gate_up(layer, n, columns):
                e, t, m = tiles[layer][n]
                hi, lo = xe[:, 0, columns], xe[:, 1, columns]
                if layer == 0:
                    h, at = HID0[e], OFF0[e] + t * P
                    g_bank, u_bank = up_bank(0, n)[0:m, 0:SLOTS], up_bank(0, n, 1)[0:m, 0:SLOTS]
                    nc.tensor.matmul(g_bank, w0[:, at:at + m], hi, start=True, stop=False)
                    nc.tensor.matmul(u_bank, w0[:, at + h:at + h + m], hi, start=True, stop=False)
                    nc.tensor.matmul(g_bank, w0[0:CL, at + 2 * h:at + 2 * h + m], lo[0:CL], start=False, stop=True)
                    return nc.tensor.matmul(u_bank, w0[CL:P, at + 2 * h:at + 2 * h + m], lo[CL:P], start=False, stop=True)
                at = e * SIZE1
                half = CL * (t // (TILES1 // 2))
                at_lo = at + HID1 + (t % (TILES1 // 2)) * P
                out_ap = up_bank(1, n)[:, 0:SLOTS]
                nc.tensor.matmul(out_ap, w0[:, at + t * P:at + (t + 1) * P], hi, start=True, stop=False)
                return nc.tensor.matmul(out_ap, w0[half:half + CL, at_lo:at_lo + P], lo[half:half + CL], start=False, stop=True)

            def down(layer, sems, n, alone):
                e, t, m = tiles[layer][n]
                if t == 0 and e >= 2:
                    pe.wait_ge(sems["y_ready"], e - 1)
                wait_hidden(pe, layer, sems, n)
                at = OFF0[e] + 3 * HID0[e] + t * C if layer == 0 else e * SIZE1 + HID1 + HID1 // 2 + t * C
                nc.tensor.matmul(y_bank(e)[0:SLOTS, 0:C], hidden[0:m, n % RING, :], w0[0:m, at:at + C],
                                 start=t == 0, stop=n + 1 == first_tile[layer][e + 1]).then_inc(sems["hidden_used"], 1)

            def combine(layer, sems, e, buf, first, last):
                pe.wait_ge(sems["y_ready"], e + 1)
                for t in range(TT):
                    ins = nc.tensor.matmul(bank[4][:, t * C:(t + 1) * C], weightedT[0:SLOTS, buf, t * P:(t + 1) * P], y_out[0:SLOTS, e % 2, :],
                                           start=first and t == 0, stop=last, skip_group_check=True)
                ins.then_inc(sems["combined"], 1)

            def turn_weighted(layer, pair):
                for e in (2 * pair, 2 * pair + 1):
                    pe.wait_ge(weighted_ready, TT * (E * layer + e + 1))
                    for t in range(TT):
                        at = (e % 2) * TOK + t * P
                        last = nc.tensor.transpose(weightedT_bank(pair)[0:SLOTS, at:at + P], weighted[:, t, e, :], ident)
                last.then_inc(weightedT_psum, 1)

            def experts(layer):
                for batch in range(2):
                    pe.wait_ge(chosen_ready, TT * (E * layer + 4 * batch + 4))
                    pe.wait_ge(xn_rounded, layer + 1)
                    pe.wait_ge(xn_split, layer + 1)
                    for c in range(2):
                        gather(bank[2 * batch + c][:, 0:4 * SLOTS], c, lambda t: chosen[:, t, 4 * batch:4 * batch + 4].rearrange("p e s -> p (e s)")).then_inc(xe_psum, 1)
                if layer == 1:
                    pe.wait_ge(gate_ready, 2)
                    for t in range(TT):
                        last = nc.tensor.transpose(bank[5][0:E, P + t * P:P + (t + 1) * P], gate[:, t, :], ident)
                    last.then_inc(combT_psum, 1)
                    pe.wait_ge(combT_ready, 1)
                    pe.wait_ge(bias_landed, 32)
                    pe.wait_ge(place_ready, 2)
                    pe.wait_ge(counts_ready, 2)
                    for t in range(TT):
                        nc.tensor.matmul(bank[4][:, t * C:(t + 1) * C], combT[0:E, t * P:(t + 1) * P], bias2[0:E, :],
                                         start=t == 0, stop=False, skip_group_check=True)
                for pair in range(3):
                    turn_weighted(layer, pair)
                pe.wait_ge(place_ready, layer + 1)
                pe.wait_ge(counts_ready, layer + 1)
                sems, ts = main[layer], tiles[layer]
                depth = 2 if layer == 0 else 4
                landed = (e0_landed, e1_landed)[layer]
                for n, (e, t, m) in enumerate(ts):
                    if t == 0:
                        pe.wait_ge(landed[e], 16)
                    if n == 0 or (e, t) == (4, 0):
                        pe.wait_ge(xe_act, 2 * layer + (1 if n == 0 else 2))
                        pe.wait_ge(xe_vec, 2 * layer + (1 if n == 0 else 2))
                    if n == 1:
                        pe.wait_ge(xe_act, 2 * layer + 2)
                        pe.wait_ge(xe_vec, 2 * layer + 2)
                    if n >= depth:
                        wait_hidden(pe, layer, sems, n - depth)
                    if n == LAG:
                        pe.wait_ge(weightedT_vec, 2 * layer + 1)
                        pe.wait_ge(weightedT_act, 2 * layer + 1)
                    gate_up(layer, n, e).then_inc(sems["up_psum"], 1)
                    if n >= LAG:
                        down(layer, sems, n - LAG, False)
                    if t == LAG + 1 and e >= 1:
                        combine(layer, sems, e - 1, e - 1, layer == 0 and e == 1, False)
                    if (e, t) == LAST_PAIR_AT:
                        pe.wait_ge(weightedT_vec, 2 * layer + 2)
                        turn_weighted(layer, 3)
                    if (e, t) == (6, 0):
                        pe.wait_ge(weightedT_act, 2 * layer + 2)
                for n in range(len(ts) - LAG, len(ts)):
                    down(layer, sems, n, False)
                combine(layer, sems, E - 1, E - 1, False, True)

                def extra(i, e):
                    sems = over[layer][i]
                    pe.wait_ge(over_chosen[layer][i], OVER_CHOSEN * (e + 1))
                    for c in range(2):
                        gather(bank[c][:, 0:SLOTS], c, lambda t: chosen[:, t, 0])
                    for t in range(TT):
                        last = nc.tensor.transpose(bank[7][0:SLOTS, t * P:(t + 1) * P], weighted[:, t, 0, :], ident)
                    last.then_inc(over_gathered[layer][i], 1)
                    pe.wait_ge(over_x[layer][i], 3 * (e + 1))
                    ns = tiles_of(layer, e)
                    for n in ns:
                        if n >= depth:
                            wait_hidden(pe, layer, sems, n - depth)
                        gate_up(layer, n, 0).then_inc(sems["up_psum"], 1)
                        if n - LAG in ns:
                            down(layer, sems, n - LAG, True)
                    for n in ns[-LAG:]:
                        down(layer, sems, n, True)
                    combine(layer, sems, e, 0, False, True)

                def skipped(i, e):
                    k = first_tile[layer][e + 1] - first_tile[layer][e]
                    sems = over[layer][i]
                    return [(over_gathered[layer][i], 1), (sems["up_psum"], k), (sems["hidden_used"], k), (sems["combined"], 1)]

                extra_passes(pe, layer, extra, skipped)

            pe.wait_ge(const_landed, 16)
            norm_T(0)
            attend(0)
            norm_T(1)
            router(0)
            places_of(0)
            experts(0)
            norm_T(2)
            attend(1)
            norm_T(3)
            router(1)
            places_of(1)
            experts(1)


def lay_out(inputs):
    import numpy as np

    f = {k: np.asarray(v) for k, v in inputs.items()}

    def heads_apart(w):
        w = w.reshape(w.shape[0], HEADS, 1, HD)
        return np.concatenate([w, w], axis=2).reshape(w.shape[0], QK)

    def layer_weights(qkv, w_out, router):
        q, k, v = qkv[:, 0:C], qkv[:, C:2 * C], qkv[:, 2 * C:3 * C]
        return np.concatenate([heads_apart(q), heads_apart(k), v, w_out, router], axis=1)

    def layer_params(b_qkv, b_out, b_gate):
        apart = heads_apart(b_qkv[None, 0:2 * C].reshape(2, C)).reshape(2 * HG, P).T
        rows = np.concatenate([b_qkv[2 * C:3 * C], b_out, b_gate])
        return np.concatenate([apart, np.broadcast_to(rows, (P, rows.size))], axis=1)

    w = np.stack([
        layer_weights(f["L0_conv_w_qkv"], f["L0_conv_w_o"], f["L0_ffn_router_W"].T),
        layer_weights(f["L1_conv_qkv_w"].T, f["L1_conv_proj_w"].T, f["L1_ffn_gate_w"].T)])
    no_bias = np.zeros((E,), np.float32)
    params = np.stack([layer_params(f["L0_conv_b_qkv"], f["L0_conv_b_o"], no_bias),
                       layer_params(f["L1_conv_qkv_b"], f["L1_conv_proj_b"], f["L1_ffn_gate_b"])], axis=1)

    rel = np.zeros((HB, SLOT, 2, REL_W), np.float32)
    for axis, name in enumerate(("L0_conv_rel_pos_h", "L0_conv_rel_pos_w")):
        for b in range(HB):
            at = SLOT * b + GRID * axis
            rel[b, 0:HD, axis, at:at + REL] = f[name][::-1].T
    key = np.arange(TOK)
    slot = np.arange(P) % SLOT
    onehot = np.where(slot[:, None] < GRID, key // GRID == slot[:, None], key % GRID == slot[:, None] - GRID)
    ranks = np.broadcast_to(np.arange(E, 0, -1), (P, E))
    masks = np.stack([slot < GRID, slot >= GRID, -1.0 * (slot >= GRID)], axis=1)
    numbers = np.arange(P)
    const = np.concatenate([np.eye(P), numbers[:, None] < numbers, np.broadcast_to(numbers + 1, (P, P)),
                            np.full((P, 1), -0.5), masks, ranks, onehot], axis=1).astype(np.float32)

    blocks = []
    for e in range(E):
        gate, up, down = f[f"L0_ffn_gate_W_{e}"].T, f[f"L0_ffn_up_W_{e}"].T, f[f"L0_ffn_down_W_{e}"].T
        down = np.pad(down, ((0, TILES0[e] * P - HID0[e]), (0, 0))).reshape(TILES0[e], P, C)
        blocks += [gate[0:P], up[0:P], np.concatenate([gate[P:C], up[P:C]]), down.transpose(1, 0, 2).reshape(P, -1)]
    experts0 = np.concatenate(blocks, axis=1)
    w1 = f["L1_ffn_w1"].transpose(2, 0, 1)
    lo = w1[P:C].reshape(CL, E, 2, HID1 // 2).transpose(2, 0, 1, 3).reshape(P, E, HID1 // 2)
    w2 = f["L1_ffn_w2"].transpose(0, 2, 1).reshape(E, TILES1, P, C).transpose(2, 0, 1, 3).reshape(P, E, TILES1 * C)
    experts1 = np.concatenate([w1[0:P], lo, w2], axis=2)
    arrays = {
        "x": f["x"].reshape(TOK, C), "weights_hi": w[:, 0:P], "weights_lo": w[:, P:C], "params": params,
        "rel": rel.reshape(P, 2, REL_W), "const": const, "experts0": experts0, "experts1": experts1,
        "bias1": f["L1_ffn_b1"].reshape(E * TILES1, P).T, "bias2": f["L1_ffn_b2"],
    }
    return {k: np.ascontiguousarray(v, dtype=np.float32) for k, v in arrays.items()}


def kernel(**inputs):
    import concourse.bacc as bacc
    from concourse.bass_utils import run_bass_kernel_spmd

    nc = bacc.Bacc("TRN2", target_bir_lowering=False, num_devices=1)
    arrays = lay_out(inputs)
    args = [nc.dram_tensor(f"{name}_dram", a.shape, F32, kind="ExternalInput").ap() for name, a in arrays.items()]
    out = nc.dram_tensor("out_dram", (TOK, C), F32, kind="ExternalOutput").ap()
    metaformer_kernel(nc, *args, out)
    result = run_bass_kernel_spmd(nc, [{f"{name}_dram": a for name, a in arrays.items()}], core_ids=[0])
    return result.results[0]["out_dram"].reshape(1, GRID, GRID, C)
```

```python
from contextlib import ExitStack

import concourse.bass as bass
import numpy as np
from concourse import mybir

P = 128
F32 = mybir.dt.float32
F32R = mybir.dt.float32r
BF16 = mybir.dt.bfloat16
ALU = mybir.AluOpType
ACT = mybir.ActivationFunctionType
AX_X = mybir.AxisListType.X

TOK = 256
TT = TOK // P
GRID = 16
C = 192
CL = C - P
HEADS = 12
HD = C // HEADS
SLOT = 32
HB = P // SLOT
HG = HEADS // HB
QK = HG * P
SCALE = float(HD) ** -0.5
SLOTS = 96
PASSES = -(-TOK // SLOTS)
JOBS = 2 * TOK // SLOTS
RING = 4
DEPTH = 4
LAG = (2, 1)
TRING = 3
REL = 2 * GRID - 1
REL_W = GRID - 1 + P
E = 8
HID0 = [432, 528, 624, 752, 896, 1088, 1312, 1584]
HID1 = 4 * C
BANK = 512

TILES0 = [-(-h // P) for h in HID0]
SIZE0 = [3 * h + n * C for h, n in zip(HID0, TILES0)]
OFF0 = [sum(SIZE0[:e]) for e in range(E + 1)]
TILES1 = HID1 // P
SIZE1 = HID1 + HID1 // 2 + TILES1 * C
W_QK, W_V, W_OUT, W_ROUTER = 0, 2 * QK, 2 * QK + C, 2 * QK + 2 * C
W_END = W_ROUTER + E
B_QK, B_V, B_O, B_GATE = 0, 2 * HG, 2 * HG + C, 2 * HG + 2 * C
B_END = B_GATE + E
CONST_W = 3 * P + 4 + E
SCRATCH = HG * TOK * 3 + (HB + TRING) * TT * TOK
KEEP_START, KEEP_SCORES, KEEP_ROUTE, KEEP_PLACE, KEEP_NORM = 16, (10, 7), 15, 3, 16
LN_EPS = [1e-6, 1e-5, 1e-6, 1e-5]


def metaformer_kernel(nc, x_in, weights_hi, weights_lo, params, rel_in, const_in, experts0, experts1,
                      bias1_in, bias2_in, out):
    with ExitStack() as ctx:
        def sb(name, shape, dtype=F32):
            return ctx.enter_context(nc.sbuf_tensor(name, [P] + shape, dtype))

        def sem(name):
            return ctx.enter_context(nc.semaphore(name))

        w0 = sb("w0", [OFF0[E]])
        att_hi = sb("att_hi", [W_END])
        att_lo = sb("att_lo", [W_END])
        par = sb("par", [2, B_END])
        rel_t = sb("rel_t", [2, REL_W])
        const = sb("const", [CONST_W])
        ident, upper = const[:, 0:P], const[:, P:2 * P]
        places = const[:, 2 * P:2 * P + SLOTS]
        small = const[:, 3 * P:CONST_W]
        ones = sb("ones", [P])
        ones_b = sb("ones_b", [P], BF16)
        upper_b = sb("upper_b", [P], BF16)
        table_of = sb("table_of", [1])
        onehot_r = sb("onehot_r", [TOK], F32R)
        bias1 = sb("bias1", [E * TILES1])
        bias2 = sb("bias2", [C])
        x = sb("x", [TT, C])
        xn = sb("xn", [TT, C + CL])
        xnT = sb("xnT", [2, TOK])
        stats = sb("stats", [TT, 6])
        mean_var = sb("mean_var", [TT, 2])
        var_eps = sb("var_eps", [TT])
        rstd = sb("rstd", [TT])
        parts = sb("parts", [6, HG, TOK], F32R)
        q_round, q_parts, k_hi, k_lo, rel_hi, rel_lo = (parts[:, i] for i in range(6))
        scratch = sb("scratch", [SCRATCH])
        used = [0]

        def carve(n):
            used[0] += n
            return scratch[:, used[0] - n:used[0]]

        qT, kT, relT = (carve(HG * TOK).rearrange("p (g t) -> p g t", g=HG) for _ in range(3))
        v1 = sb("v1", [TT, HEADS, SLOT])
        neg_max = sb("neg_max", [HEADS, TT])
        probs_room = carve(HB * TT * TOK)
        probs = probs_room.rearrange("p (h t k) -> p h t k", h=HB, t=TT)
        onehot = probs_room[:, 0:TOK]
        probsT = carve(TRING * TT * TOK).rearrange("p (h k t) -> p h k t", h=TRING, k=TT)
        o_sum = sb("o_sum", [TT, HEADS])
        o_tok = sb("o_tok", [TT, C])
        oT = sb("oT", [2, TOK])
        used[0] = 0
        chosen = parts[:].rearrange("p a g t -> p (a g t)")[:, 0:TT * E * SLOTS].rearrange("p (t e s) -> p t e s", t=TT, e=E)
        xn_parts = parts[:].rearrange("p a g t -> p (a g t)")[:, TT * E * SLOTS:TT * E * SLOTS + 2 * TT * (C + CL)]
        xn_hi, xn_lo = (a.rearrange("p (t c) -> p t c", t=TT) for a in (xn_parts[:, 0:TT * (C + CL)], xn_parts[:, TT * (C + CL):]))
        weighted = carve(TT * E * SLOTS).rearrange("p (t e s) -> p t e s", t=TT, e=E)
        weightedT = carve(E * TOK).rearrange("p (e t) -> p e t", e=E)
        xe_hi = carve(E * SLOTS).rearrange("p (e s) -> p e s", e=E)
        hidden = carve(RING * 2 * SLOTS).rearrange("p (r u s) -> p r u s", r=RING, u=2)
        silu_g = carve(2 * SLOTS).rearrange("p (r s) -> p r s", r=2)
        y_out = carve(2 * C).rearrange("p (r c) -> p r c", r=2)
        xe_lo = sb("xe_lo", [E, 2, SLOTS])
        used_w0 = [E * SIZE1]

        def carve_w0(*shape):
            n = int(np.prod(shape))
            used_w0[0] += n
            names = "abc"[:len(shape)]
            return w0[:, used_w0[0] - n:used_w0[0]].rearrange(f"p ({' '.join(names)}) -> p {' '.join(names)}", **dict(zip(names, shape)))

        JOB_ROOMS = 2
        job_weights_at = [used_w0[0] + i * SIZE1 for i in range(JOB_ROOMS)]
        carve_w0(JOB_ROOMS, SIZE1)
        job_weighted = carve_w0(JOBS, TT, SLOTS)
        job_weightedT = carve_w0(JOBS, TOK)
        job_xe_hi = carve_w0(JOBS, SLOTS)
        job_xe_lo = carve_w0(JOBS, 2 * SLOTS).rearrange("p j (u s) -> p j u s", u=2)
        keys = carve_w0(PASSES - 1, E)
        job_key = carve_w0(JOBS)
        job_expert = carve_w0(JOBS)
        job_base = carve_w0(JOBS)
        job_is = carve_w0(JOBS, E)
        job_place = carve_w0(TT, JOBS)
        job_gate = carve_w0(TT, JOBS)
        job_bias = carve_w0(JOBS, TILES1)
        job_tmp = carve_w0(JOBS * TILES1 * E)
        job_number = carve_w0(1 + JOBS)
        job_chosen = parts[:].rearrange("p a g t -> p (a g t)")[:, TT * E * SLOTS + 2 * TT * (C + CL):][:, 0:JOBS * TT * SLOTS].rearrange(
            "p (j t s) -> p j t s", j=JOBS, t=TT)
        job_regs = ctx.enter_context(nc.sbuf_tensor("job_regs", [1, 1 + JOBS], mybir.dt.int32))
        count = sb("count", [E])
        place = sb("place", [TT, E])
        over_place = sb("over_place", [TT])
        counts = ctx.enter_context(nc.sbuf_tensor("counts", [1, E + 1], mybir.dt.int32))
        acc = xn[:, :, 0:C]
        logit = sb("logit", [TT, E])
        ex = sb("ex", [TT, E])
        gate = sb("gate", [TT, E])
        picks = sb("picks", [TT, E])
        ranked = sb("ranked", [TT, E])
        mask = sb("mask", [TT, E], BF16)
        router_sum = sb("router_sum", [E])
        red = sb("red", [6, TT])
        neg_top, total, top, rank_top = (red[:, i] for i in range(4))
        tmp = sb("tmp", [TT, E])
        combT = oT[:, 0, :]

        bank = [ctx.enter_context(nc.psum_tensor(f"bank{i}", [P, BANK], F32)) for i in range(8)]

        x_landed, const_landed, par_landed, rel_landed = (sem(s) for s in ("x_landed", "const_landed", "par_landed", "rel_landed"))
        att_landed = [sem(f"att_landed{i}") for i in range(2)]
        e0_landed = [sem(f"e0_landed{i}") for i in range(E)]
        e1_landed = [sem(f"e1_landed{i}") for i in range(E)]
        bias_landed = sem("bias_landed")
        ones_set, zeros_set = sem("ones_set"), sem("zeros_set")
        vec_step = sem("vec_step")
        stats_ready, rstd_ready, xn_ready = sem("stats_ready"), sem("rstd_ready"), sem("xn_ready")
        xnT_psum, xnT_act, xnT_vec = sem("xnT_psum"), sem("xnT_act"), sem("xnT_vec")
        q_psum, k_psum, v_psum, rel_psum = sem("q_psum"), sem("k_psum"), sem("v_psum"), sem("rel_psum")
        q_ready, q_rounded, q_split = sem("q_ready"), sem("q_rounded"), sem("q_split")
        k_ready, k_rounded, k_split, v_ready = sem("k_ready"), sem("k_rounded"), sem("k_split"), sem("v_ready")
        rel_half, rel_ready, rel_rounded, rel_split = sem("rel_half"), sem("rel_ready"), sem("rel_rounded"), sem("rel_split")
        scores_psum, max_ready, probs_ready = sem("scores_psum"), sem("max_ready"), sem("probs_ready")
        probsT_psum, probsT_vec, probsT_act = sem("probsT_psum"), sem("probsT_vec"), sem("probsT_act")
        o_copied, o_turned = sem("o_copied"), sem("o_turned")
        o_psum, o_ready, oT_psum, oT_ready = sem("o_psum"), sem("o_ready"), sem("oT_psum"), sem("oT_ready")
        proj_psum, x_added, x_ready = sem("proj_psum"), sem("x_added"), sem("x_ready")
        router_sum_psum = sem("router_sum_psum")
        logit_psum, logit_ready, exp_ready = sem("logit_psum"), sem("logit_ready"), sem("exp_ready")
        gate_ready = sem("gate_ready")
        combT_psum, combT_ready, bias2_psum = sem("combT_psum"), sem("combT_ready"), sem("bias2_psum")
        acc_ready = sem("acc_ready")
        xn_rounded, xn_split = sem("xn_rounded"), sem("xn_split")
        picked, place_psum, place_ready, counts_ready = sem("picked"), sem("place_psum"), sem("place_ready"), sem("counts_ready")
        chosen_ready, weighted_ready = sem("chosen_ready"), sem("weighted_ready")
        xe_psum, xe_act, xe_vec = sem("xe_psum"), sem("xe_act"), sem("xe_vec")
        weightedT_psum, weightedT_act, weightedT_vec = sem("weightedT_psum"), sem("weightedT_act"), sem("weightedT_vec")
        moe_done = sem("moe_done")

        def stream_sems(name):
            return {s: sem(f"{s}_{name}") for s in
                    ("up_psum", "silu_ready", "hidden_vec", "hidden_act", "hidden_used", "y_ready", "combined")}

        main = [stream_sems(f"main{layer}") for layer in range(2)]
        over = [None] + [stream_sems(f"over{i}") for i in range(1, PASSES)]
        over_chosen, over_gathered, over_x = ([None] + [sem(f"{s}{i}") for i in range(1, PASSES)]
                                              for s in ("over_chosen", "over_gathered", "over_x"))
        zeros_job, jobs_ready, job_picked, job_gathered, job_x = (
            sem(s) for s in ("zeros_job", "jobs_ready", "job_picked", "job_gathered", "job_x"))
        job_landed = [sem(f"job_landed{k}") for k in range(JOBS)]
        out_landed = sem("out_landed")

        STEPS1 = TILES1 // 2
        steps0 = [(e, t, min(P, HID0[e] - t * P)) for e in range(E) for t in range(TILES0[e])]
        steps1 = [(e, t, P) for e in range(E + JOBS) for t in range(STEPS1)]
        steps_of_layer = (steps0, steps1)
        first_step = [[next(n for n, step in enumerate(ss) if step[0] == e) for e in range(ss[-1][0] + 1)] + [len(ss)]
                      for ss in steps_of_layer]
        main_steps = [range(first_step[layer][E]) for layer in range(2)]

        def hidden_by_act(layer, n):
            return layer == 1 and n % 2 == 1

        def hidden_counts(layer, n):
            act = n // 2 if layer == 1 else 0
            return n - act, act

        def wait_hidden(eng, layer, sems, n):
            vec, act = hidden_counts(layer, n + 1)
            if hidden_by_act(layer, n):
                eng.wait_ge(sems["hidden_act"], act)
            else:
                eng.wait_ge(sems["hidden_vec"], vec)

        def up_bank(n):
            return bank[n % DEPTH][:, 0:2 * SLOTS].rearrange("p (u s) -> p u s", u=2)

        PAIR_AT = ((0, 0), (0, 1), (1, 0), (2, 0))

        OVER_CHOSEN = 1 + 2 * TT
        OVER_X = 4

        def weightedT_bank(pair):
            return bank[(7, 6, 7, 7)[pair]]

        def y_bank(e):
            return bank[5 + e % 2]

        PICK_JOB_AT, GATHER_JOB_AT, COPY_JOB_AT = (4, 1), (5, 2), (6, 0)

        def xn_count(n):
            return TT * (n + 1 + (n + 1) // 2)

        def largest_count(eng):
            eng.wait_ge(counts_ready, 1)
            return eng.value_load(counts[0:1, E:E + 1], min_val=0, max_val=TOK)

        def extra_passes(eng, most, body, skipped):
            for i in range(1, PASSES):
                with eng.If(most > i * SLOTS):
                    for e in range(E):
                        n = eng.value_load(counts[0:1, e:e + 1], min_val=0, max_val=TOK)
                        with eng.If(n > i * SLOTS):
                            body(i, e)
                        with eng.Else():
                            for s, k in skipped(i, e):
                                if k:
                                    eng.drain().then_inc(s, k)

        def jobs(eng, body, otherwise):
            eng.wait_ge(jobs_ready, 1)
            number = eng.value_load(job_regs[0:1, 0:1], min_val=0, max_val=JOBS)

            def rest(k):
                if k == JOBS:
                    otherwise(k)
                    return
                with eng.If(number > k):
                    body(k)
                    rest(k + 1)
                with eng.Else():
                    otherwise(k)

            rest(0)

        def tokens_of(e):
            return (xe_hi[:, e], xe_lo[:, e]) if e < E else (job_xe_hi[:, e - E], job_xe_lo[:, e - E])

        def bias1_of(e, u, t):
            at = u * STEPS1 + t
            return bias1[:, e * TILES1 + at:e * TILES1 + at + 1] if e < E else job_bias[:, e - E, at:at + 1]

        def steps_of(layer, e):
            return range(first_step[layer][e], first_step[layer][e + 1])

        def turned_by_act(n):
            return n % 3 == 2

        def wait_probsT(eng, n):
            if turned_by_act(n):
                eng.wait_ge(probsT_act, (n + 1) // 3)
            else:
                eng.wait_ge(probsT_vec, n + 1 - (n + 1) // 3)

        block = ctx.enter_context(nc.Block())

        @block.sync
        def _(sp):
            sp.dma_start(x[:], x_in.rearrange("(t p) c -> p t c", p=P)).then_inc(x_landed, 16)
            sp.dma_start(const[:], const_in[:, 0:CONST_W]).then_inc(const_landed, 16)
            sp.dma_start(att_hi[:], weights_hi[0]).then_inc(att_landed[0], 16)
            sp.dma_start(att_lo[0:CL, :], weights_lo[0]).then_inc(att_landed[0], 16)
            sp.dma_start(par[:], params).then_inc(par_landed, 16)
            sp.dma_start(rel_t[:], rel_in).then_inc(rel_landed, 16)
            sp.dma_start(onehot[:], const_in[:, CONST_W:CONST_W + TOK]).then_inc(rel_landed, 16)
            sp.dma_start(bias1[:], bias1_in).then_inc(bias_landed, 16)
            sp.dma_start(bias2[0:E, :], bias2_in).then_inc(bias_landed, 16)
            for e in range(E):
                sp.dma_start(w0[:, OFF0[e]:OFF0[e + 1]], experts0[:, OFF0[e]:OFF0[e + 1]]).then_inc(e0_landed[e], 16)
            sp.wait_ge(logit_psum, 1)
            sp.dma_start(att_hi[:], weights_hi[1]).then_inc(att_landed[1], 16)
            sp.dma_start(att_lo[0:CL, :], weights_lo[1]).then_inc(att_landed[1], 16)
            sp.wait_ge(moe_done, TT)
            for e in range(E):
                sp.dma_start(w0[:, e * SIZE1:(e + 1) * SIZE1], experts1[:, e]).then_inc(e1_landed[e], 16)

            def load_job(k):
                expert = sp.value_load(job_regs[0:1, 1 + k:2 + k], min_val=0, max_val=E - 1)
                if k >= JOB_ROOMS:
                    sp.wait_ge(main[1]["hidden_used"], first_step[1][E + k - JOB_ROOMS + 1])
                at = job_weights_at[k % JOB_ROOMS]
                sp.dma_start(w0[:, at:at + SIZE1], experts1[:, bass.ds(expert, 1), :].rearrange("p e c -> p (e c)")).then_inc(job_landed[k], 16)

            jobs(sp, load_job, lambda k: None)
            sp.wait_ge(x_ready, 4)
            sp.dma_start(out.rearrange("(t p) c -> p t c", p=P), x[:]).then_inc(out_landed, 16)
            sp.wait_ge(out_landed, 16)

        @block.gpsimd
        def _(pool):
            nc.gpsimd.memset(v1[:, :, :, HD:HD + 1], 1.0).then_inc(ones_set, 1)
            nc.gpsimd.memset(v1[:, :, :, HD + 1:SLOT], 0.0).then_inc(ones_set, 1)
            nc.gpsimd.memset(ones[:], 1.0).then_inc(ones_set, 1)
            pool.wait_ge(ones_set, 3)
            nc.gpsimd.memset(xe_lo[CL:P, :, 0, :], 0.0).then_inc(zeros_set, 1)
            pool.wait_ge(zeros_set, 1)
            nc.gpsimd.memset(xe_lo[0:CL, :, 1, :], 0.0).then_inc(zeros_set, 1)
            pool.wait_ge(zeros_set, 2)
            pool.wait_ge(const_landed, 16)
            for n in range(4):
                pool.wait_ge(stats_ready, n + 1)
                nc.gpsimd.tensor_tensor(rstd[:], var_eps[:], small[:, 0:1].to_broadcast([P, TT]), ALU.pow).then_inc(rstd_ready, 1)
                if n == 0:
                    pool.wait_ge(rel_landed, 32)
                    nc.gpsimd.tensor_copy(onehot_r[:], onehot[:]).then_inc(ones_set, 1)
                    nc.gpsimd.tensor_copy(ones_b[:], ones[:]).then_inc(ones_set, 1)
                    nc.gpsimd.tensor_copy(upper_b[:], upper).then_inc(ones_set, 1)
                if n % 2 == 0:
                    layer = n // 2
                    for g in range(HG):
                        pool.wait_ge(k_ready, HG * layer + g + 1)
                        pool.wait_ge(k_rounded, HG * layer + g + 1)
                        nc.gpsimd.tensor_tensor(k_lo[:, g], kT[:, g], k_hi[:, g].bitcast(F32), ALU.subtract).then_inc(k_split, 1)
                    if layer == 0:
                        for g in range(HG):
                            pool.wait_ge(rel_ready, 2 * (g + 1))
                            pool.wait_ge(rel_rounded, g + 1)
                            nc.gpsimd.tensor_tensor(rel_lo[:, g], relT[:, g], rel_hi[:, g].bitcast(F32), ALU.subtract).then_inc(rel_split, 1)
                else:
                    layer = n // 2
                    pool.wait_ge(xn_ready, xn_count(n))
                    pool.wait_ge(xn_rounded, layer + 1)
                    nc.gpsimd.tensor_tensor(xn_lo, xn[:], xn_hi.bitcast(F32), ALU.subtract).then_inc(xn_split, 1)
                    if layer == 0:
                        pool.wait_ge(xn_split, 1)
                        pool.wait_ge(xnT_psum, 2)
                        nc.gpsimd.tensor_tensor(acc, x[:], acc, ALU.add).then_inc(acc_ready, 1)
                    pool.wait_ge(place_ready, layer + 1)
                    pool.wait_ge(gate_ready, layer + 1)
                    pool.wait_ge(probsT_psum, (layer + 1) * HEADS)
                    if layer == 1:
                        pool.wait_ge(xn_split, 2)
                        nc.gpsimd.memset(job_xe_lo, 0.0).then_inc(zeros_job, 1)
                        pool.wait_ge(zeros_job, 1)
                    for e in range(E):
                        for t in range(TT):
                            nc.gpsimd.tensor_scalar(weighted[:, t, e, :], places, place[:, t, e:e + 1], gate[:, t, e:e + 1],
                                                    ALU.is_equal, ALU.mult).then_inc(weighted_ready, 1)

        @block.scalar
        def _(act):
            def norm_T(n):
                act.wait_ge(xnT_psum, n + 1)
                nc.scalar.copy(xnT[:, 0, :], bank[6][:, 0:TOK]).then_inc(xnT_act, 1)

            def load_table(func):
                nc.scalar.activation(table_of[0:1, :], ones[0:1, 0:1], func)

            def copy_o(layer, g):
                act.wait_ge(o_psum, layer * HEADS + (g + 1) * HB)
                act.wait_ge(q_split, HG * (layer + 1))
                nc.scalar.copy(qT[:, g, :], bank[6 + g % 2][:, 0:TOK]).then_inc(o_copied, 1)

            def copy_weightedT(layer, pair):
                act.wait_ge(weightedT_psum, 4 * layer + pair + 1)
                nc.scalar.copy(weightedT[0:SLOTS, 2 * pair:2 * pair + 2].rearrange("p e t -> p (e t)"),
                               weightedT_bank(pair)[0:SLOTS, :]).then_inc(weightedT_act, 1)

            def stream(layer, sems, ns, main_layer=None):
                for n in ns:
                    e, t, m = steps_of_layer[layer][n]
                    if layer == 0:
                        act.wait_ge(sems["up_psum"], n + 1)
                        if n >= 2:
                            wait_hidden(act, 0, sems, n - 2)
                        nc.scalar.activation(silu_g[0:m, n % 2, :], up_bank(n)[0:m, 0], ACT.Silu).then_inc(sems["silu_ready"], 1)
                    elif hidden_by_act(layer, n):
                        act.wait_ge(sems["up_psum"], n + 1)
                        if n >= RING:
                            act.wait_ge(sems["hidden_used"], n - RING + 1)
                        for u in range(2):
                            ins = nc.scalar.activation(hidden[:, n % RING, u], up_bank(n)[:, u], ACT.Relu, bias=bias1_of(e, u, t))
                        ins.then_inc(sems["hidden_act"], 1)
                    if main_layer is not None and (e, t) in PAIR_AT[1::2]:
                        copy_weightedT(layer, PAIR_AT.index((e, t)))

            act.wait_ge(ones_set, 3)
            load_table(ACT.Exp)
            act.wait_ge(par_landed, 16)
            for layer in range(2):
                norm_T(2 * layer)
                act.wait_ge(q_psum, layer + 1)
                order = [(g, which) for which in range(2) for g in range(HG)] if layer == 0 else [(g, which) for g in range(HG) for which in range(2)]
                for g, which in order:
                    part, done = ((qT, q_ready), (q_round, q_rounded))[which]
                    nc.scalar.activation(part[:, g, :], bank[2 + g // 2][:, (g % 2) * TOK:(g % 2 + 1) * TOK], ACT.Identity,
                                         bias=par[:, layer, B_QK + g:B_QK + g + 1]).then_inc(done, 1)
                if layer == 0:
                    act.wait_ge(rel_psum, 1)
                    for half in range(2):
                        rows = relT[:].rearrange("p g (r c) -> p r g c", c=GRID)[:, 8 * half:8 * half + 8]
                        nc.scalar.activation(rows, bank[5 + half][:, 0:HG * P].rearrange("p (r g c) -> p r g c", r=8, g=HG),
                                             ACT.Copy, scale=small[:, 1:2]).then_inc(rel_half, 1)
                for h in range(HEADS + 2):
                    if h < HEADS:
                        head = layer * HEADS + h
                        act.wait_ge(max_ready, head + 1)
                        if head >= HB:
                            act.wait_ge(probsT_psum, head - HB + 1)
                        if h == 0 and layer == 0:
                            act.wait_ge(ones_set, 4)
                        if h == 0 and layer == 1:
                            act.wait_ge(moe_done, TT)
                        for t in range(TT):
                            nc.scalar.activation(probs[:, h % HB, t, :], bank[h % HB][:, t * TOK:(t + 1) * TOK], ACT.Exp,
                                                 bias=neg_max[:, h, t:t + 1]).then_inc(probs_ready, 1)
                    if h >= 2 and turned_by_act(layer * HEADS + h - 2):
                        head = layer * HEADS + h - 2
                        act.wait_ge(probsT_psum, head + 1)
                        if head >= TRING:
                            act.wait_ge(o_psum, head - TRING + 1)
                        nc.scalar.copy(probsT[:, head % TRING], bank[4 + head % 2][:]).then_inc(probsT_act, 1)
                    if h >= HB + 3 and (h - 3) % HB == 0:
                        copy_o(layer, (h - 3) // HB - 1)
                copy_o(layer, HG - 1)
                act.wait_ge(oT_psum, 2 * layer + 1)
                nc.scalar.copy(oT[:, 0, :], bank[7][:, 0:TOK]).then_inc(oT_ready, 1)
                act.wait_ge(oT_psum, 2 * layer + 2)
                nc.scalar.copy(oT[0:CL, 1, :], bank[2][0:CL, 0:TOK]).then_inc(oT_ready, 1)
                norm_T(2 * layer + 1)
                for t in range(TT):
                    act.wait_ge(logit_ready, TT * layer + t + 1)
                    nc.scalar.activation(ex[:, t], logit[:, t], ACT.Exp, bias=neg_top[:, t:t + 1],
                                         accum_out=total[:, t:t + 1]).then_inc(exp_ready, 1)
                if layer == 0:
                    load_table(ACT.Silu)
                act.wait_ge(o_psum, (layer + 1) * HEADS)
                for batch in range(2):
                    act.wait_ge(xe_psum, 4 * layer + 2 * batch + 1)
                    nc.scalar.copy(xe_hi[:, 4 * batch:4 * batch + 4], bank[2 * batch][:, 0:4 * SLOTS].rearrange("p (e s) -> p e s", e=4)).then_inc(xe_act, 1)
                if layer == 1:
                    act.wait_ge(bias_landed, 32)
                if layer == 0:
                    most = largest_count(act)
                stream(layer, main[layer], main_steps[layer], layer)
                if layer == 0:
                    extra_passes(act, most, lambda i, e: stream(0, over[i], steps_of(0, e)),
                                 lambda i, e: [(over[i]["silu_ready"], len(steps_of(0, e)))])
                    load_table(ACT.Exp)
                else:
                    jobs(act, lambda k: stream(1, main[1], steps_of(1, E + k)), lambda k: None)

        @block.vector
        def _(dve):
            steps = [0]

            def step(ins):
                steps[0] += 1
                ins.then_inc(vec_step, 1)
                dve.wait_ge(vec_step, steps[0])

            def tick(ins):
                steps[0] += 1
                ins.then_inc(vec_step, 1)
                return steps[0]

            def norm(n):
                done = [0] * TT
                for t in range(TT):
                    if n % 2 == 1:
                        dve.wait_ge(x_added, TT * (n // 2) + t + 1)
                    if n == 2:
                        dve.wait_ge(moe_done, t + 1)
                    done[t] = tick(nc.vector.bn_stats(stats[:, t, :], x[:, t, :]))
                for t in range(TT):
                    dve.wait_ge(vec_step, done[t])
                    done[t] = tick(nc.vector.bn_aggr(mean_var[:, t, :], stats[:, t, :]))
                dve.wait_ge(vec_step, done[TT - 1])
                nc.vector.tensor_scalar(var_eps[:], mean_var[:, :, 1], LN_EPS[n], None, ALU.add).then_inc(stats_ready, 1)
                if n % 2 == 1:
                    dve.wait_ge(xnT_psum, n + 1)
                    nc.vector.tensor_copy(xnT[0:CL, 1, :], bank[7][0:CL, 0:TOK]).then_inc(xnT_vec, 1)
                dve.wait_ge(rstd_ready, n + 1)
                for t in range(TT):
                    nc.vector.tensor_scalar(xn[:, t, 0:C], x[:, t, :], mean_var[:, t, 0:1], rstd[:, t:t + 1],
                                            ALU.subtract, ALU.mult).then_inc(xn_ready, 1)
                    if n % 2 == 1:
                        nc.vector.tensor_scalar(xn[:, t, C:C + CL], x[:, t, P:C], mean_var[:, t, 0:1], rstd[:, t:t + 1],
                                                ALU.subtract, ALU.mult).then_inc(xn_ready, 1)
                if n % 2 == 0:
                    dve.wait_ge(xnT_psum, n + 1)
                    nc.vector.tensor_copy(xnT[0:CL, 1, :], bank[7][0:CL, 0:TOK]).then_inc(xnT_vec, 1)

            def attend(layer):
                dve.wait_ge(k_psum, layer + 1)
                if layer == 1:
                    dve.wait_ge(scores_psum, HEADS)
                for g in range(HG):
                    for part, done in ((k_hi, k_rounded), (kT, k_ready)):
                        nc.vector.tensor_scalar(part[:, g, :], bank[g // 2][:, (g % 2) * TOK:(g % 2 + 1) * TOK],
                                                par[:, layer, B_QK + HG + g:B_QK + HG + g + 1], SCALE,
                                                ALU.add, ALU.mult).then_inc(done, 1)
                for g in range(HG):
                    dve.wait_ge(q_ready, HG * layer + g + 1)
                    dve.wait_ge(q_rounded, HG * layer + g + 1)
                    nc.vector.scalar_tensor_tensor(q_parts[:, g], q_round[:, g].bitcast(F32), small[:, 3:4], qT[:, g],
                                                   ALU.mult, ALU.add).then_inc(q_split, 1)
                    if g == 0:
                        dve.wait_ge(v_psum, layer + 1)
                        for t in range(TT):
                            nc.vector.tensor_tensor(v1[:, t, :, 0:HD], bank[4][:, t * C:(t + 1) * C].rearrange("p (h d) -> p h d", d=HD),
                                                    par[:, layer, B_V:B_V + C].rearrange("p (h d) -> p h d", d=HD), ALU.add).then_inc(v_ready, 1)
                if layer == 0:
                    dve.wait_ge(rel_psum, 2)
                    dve.wait_ge(rel_half, 2)
                    for g in range(HG):
                        for half, b in enumerate((7, 3)):
                            cols = relT[:, g, :].rearrange("p (r c) -> p c r", c=GRID)[:, 8 * half:8 * half + 8]
                            new = bank[b][:, 0:HG * P].rearrange("p (c g r) -> p c g r", c=8, g=HG)[:, :, g]
                            nc.vector.scalar_tensor_tensor(cols, new, small[:, 2:3], cols, ALU.mult, ALU.add).then_inc(rel_ready, 1)
                        dve.wait_ge(rel_ready, 2 * (g + 1))
                        nc.vector.tensor_copy(rel_hi[:, g], relT[:, g]).then_inc(rel_rounded, 1)
                for h in range(HEADS + 2):
                    if h < HEADS:
                        dve.wait_ge(scores_psum, layer * HEADS + h + 1)
                        nc.vector.tensor_reduce(neg_max[:, h, :], bank[h % HB][:].rearrange("p (t k) -> p t k", t=TT),
                                                AX_X, ALU.max, negate=True).then_inc(max_ready, 1)
                    if h >= 2 and not turned_by_act(layer * HEADS + h - 2):
                        head = layer * HEADS + h - 2
                        dve.wait_ge(probsT_psum, head + 1)
                        if head >= TRING:
                            dve.wait_ge(o_psum, head - TRING + 1)
                        nc.vector.tensor_copy(probsT[:, head % TRING], bank[4 + head % 2][:]).then_inc(probsT_vec, 1)
                def normalise(part, heads):
                    dve.wait_ge(o_turned, 2 * layer + part + 1)
                    n = heads.stop - heads.start
                    for t in range(TT):
                        o = bank[t][:, 0:QK].rearrange("p (h d) -> p h d", d=SLOT)[:, heads]
                        step(nc.vector.reciprocal(o_sum[:, t, heads], o[:, :, HD]))
                        nc.vector.tensor_tensor(o_tok[:, t, HD * heads.start:HD * heads.stop].rearrange("p (h d) -> p h d", d=HD), o[:, :, 0:HD],
                                                o_sum[:, t, heads].unsqueeze(2).to_broadcast([P, n, HD]), ALU.mult).then_inc(o_ready, 1)

                normalise(0, slice(0, 2 * HB))
                dve.wait_ge(router_sum_psum, layer + 1)
                nc.vector.tensor_scalar(router_sum[:], bank[5][:, TT * E:(TT + 1) * E], -1.0, None, ALU.mult)
                normalise(1, slice(2 * HB, HEADS))
                for t in range(TT):
                    step(nc.vector.tensor_tensor(x[:, t, :], x[:, t, :], par[:, layer, B_O:B_O + C], ALU.add))
                dve.wait_ge(proj_psum, layer + 1)
                for t in range(TT):
                    nc.vector.tensor_tensor(x[:, t, :], x[:, t, :], bank[4][:, t * C:(t + 1) * C], ALU.add).then_inc(x_added, 1)

            def round_xn(layer):
                dve.wait_ge(xn_ready, xn_count(2 * layer + 1))
                dve.wait_ge(scores_psum, (layer + 1) * HEADS)
                nc.vector.tensor_copy(xn_hi, xn[:]).then_inc(xn_rounded, 1)

            def route(layer):
                dve.wait_ge(logit_psum, layer + 1)
                done = [steps[0]] * TT

                def both(make):
                    for t in range(TT):
                        dve.wait_ge(vec_step, done[t])
                        done[t] = tick(make(t))

                both(lambda t: nc.vector.scalar_tensor_tensor(logit[:, t], router_sum[:], mean_var[:, t, 0:1], bank[5][:, t * E:(t + 1) * E],
                                                              ALU.mult, ALU.add))
                both(lambda t: nc.vector.scalar_tensor_tensor(logit[:, t], logit[:, t], rstd[:, t:t + 1], par[:, layer, B_GATE:B_GATE + E],
                                                              ALU.mult, ALU.add))
                for t in range(TT):
                    dve.wait_ge(vec_step, done[t])
                    nc.vector.tensor_reduce(neg_top[:, t:t + 1], logit[:, t], AX_X, ALU.max, negate=True).then_inc(logit_ready, 1)
                for t in range(TT):
                    dve.wait_ge(exp_ready, TT * layer + t + 1)
                    done[t] = tick(nc.vector.reciprocal(total[:, t:t + 1], total[:, t:t + 1]))
                both(lambda t: nc.vector.tensor_scalar(gate[:, t], ex[:, t], total[:, t:t + 1], None, ALU.mult))
                rank = small[:, 4:4 + E]
                for k, values in enumerate((gate, tmp)):
                    both(lambda t: nc.vector.tensor_reduce(top[:, t:t + 1], values[:, t], AX_X, ALU.max))
                    both(lambda t: nc.vector.scalar_tensor_tensor(ranked[:, t], values[:, t], top[:, t:t + 1], rank, ALU.is_equal, ALU.mult))
                    both(lambda t: nc.vector.tensor_reduce(rank_top[:, t:t + 1], ranked[:, t], AX_X, ALU.max))
                    if k == 0:
                        both(lambda t: nc.vector.tensor_scalar(picks[:, t], ranked[:, t], rank_top[:, t:t + 1], None, ALU.is_equal))
                        both(lambda t: nc.vector.scalar_tensor_tensor(tmp[:, t], picks[:, t], -2.0, gate[:, t], ALU.mult, ALU.add))
                for t in range(TT):
                    dve.wait_ge(vec_step, done[t])
                    nc.vector.scalar_tensor_tensor(mask[:, t], ranked[:, t], rank_top[:, t:t + 1], picks[:, t], ALU.is_equal, ALU.add).then_inc(picked, 1)
                dve.wait_ge(picked, TT * (layer + 1))
                last = nc.vector.tensor_tensor(gate[:], gate[:], mask[:], ALU.mult)
                if layer == 1:
                    step(last)
                    step(nc.vector.tensor_reduce(red[:, 4], gate[:], AX_X, ALU.add))
                    step(nc.vector.reciprocal(red[:, 5], red[:, 4]))
                    last = nc.vector.tensor_tensor(gate[:], gate[:], red[:, 5].unsqueeze(2).to_broadcast([P, TT, E]), ALU.mult)
                last.then_inc(gate_ready, 1)
                dve.wait_ge(place_psum, layer + 1)
                nc.vector.scalar_tensor_tensor(place[:], bank[4][:, 0:TT * E].rearrange("p (t e) -> p t e", e=E), 1.0, mask[:],
                                               ALU.add, ALU.mult).then_inc(place_ready, 1)
                dve.wait_ge(place_ready, layer + 1)

            def copy_weightedT(layer, pair):
                dve.wait_ge(weightedT_psum, 4 * layer + pair + 1)
                nc.vector.tensor_copy(weightedT[0:SLOTS, 2 * pair:2 * pair + 2].rearrange("p e t -> p (e t)"),
                                      weightedT_bank(pair)[0:SLOTS, :]).then_inc(weightedT_vec, 1)

            def copy_y(sems, e):
                if e >= 2:
                    dve.wait_ge(sems["combined"], e - 1)
                nc.vector.tensor_copy(y_out[0:SLOTS, e % 2, :], y_bank(e)[0:SLOTS, 0:C]).then_inc(sems["y_ready"], 1)

            def stream(layer, sems, ns, end):
                for n in ns:
                    e, t, m = steps_of_layer[layer][n]
                    if not hidden_by_act(layer, n):
                        dve.wait_ge(sems["silu_ready"] if layer == 0 else sems["up_psum"], n + 1)
                        if n >= RING:
                            dve.wait_ge(sems["hidden_used"], n - RING + 1)
                    if layer == 0:
                        nc.vector.tensor_tensor(hidden[0:m, n % RING, 0], silu_g[0:m, n % 2, :], up_bank(n)[0:m, 1], ALU.mult).then_inc(sems["hidden_vec"], 1)
                    elif not hidden_by_act(layer, n):
                        for u in range(2):
                            ins = nc.vector.tensor_scalar(hidden[:, n % RING, u], up_bank(n)[:, u], bias1_of(e, u, t), 0.0, ALU.add, ALU.max)
                        ins.then_inc(sems["hidden_vec"], 1)
                    if t == LAG[layer] and n - t - 1 in ns:
                        dve.wait_ge(sems["hidden_used"], n - t)
                        copy_y(sems, e - 1)
                    if end == "main" and (e, t) in PAIR_AT[0::2]:
                        copy_weightedT(layer, PAIR_AT.index((e, t)))
                    if end == "main" and layer == 1:
                        if (e, t) == (1, 1):
                            list_jobs()
                        if (e, t) == (2, 1):
                            number_jobs()
                        if (e, t) == (3, 1):
                            place_jobs()
                        if (e, t) == PICK_JOB_AT:
                            pick_job(0)
                        if (e, t) == COPY_JOB_AT:
                            copy_job(0)
                e = steps_of_layer[layer][ns[-1]][0]
                dve.wait_ge(sems["hidden_used"], ns[-1] + 1)
                copy_y(sems, e)

            def list_jobs():
                for i in range(PASSES - 1):
                    step(nc.vector.scalar_tensor_tensor(keys[:, i], count[:], float((i + 1) * SLOTS), places[:, i * E:(i + 1) * E],
                                                        ALU.is_gt, ALU.mult))
                every = keys.rearrange("p a b -> p (a b)")
                for k in range(JOBS):
                    step(nc.vector.tensor_reduce(job_key[:, k:k + 1], every, AX_X, ALU.max))
                    step(nc.vector.scalar_tensor_tensor(every, every, job_key[:, k:k + 1], every, ALU.not_equal, ALU.mult))

            def number_jobs():
                step(nc.vector.tensor_scalar(job_base, job_key, float(E), None, ALU.is_gt))
                step(nc.vector.scalar_tensor_tensor(job_expert, job_base, -float(E), job_key, ALU.mult, ALU.add))
                step(nc.vector.tensor_scalar(job_base, job_base, 1.0, float(SLOTS), ALU.add, ALU.mult))
                step(nc.vector.tensor_tensor(job_is, places[:, 0:E].unsqueeze(1).to_broadcast([P, JOBS, E]),
                                             job_expert.unsqueeze(2).to_broadcast([P, JOBS, E]), ALU.is_equal))
                step(nc.vector.tensor_scalar(job_number[:, 1:1 + JOBS], job_key, 0.0, None, ALU.is_gt))
                step(nc.vector.tensor_reduce(job_number[:, 0:1], job_number[:, 1:1 + JOBS], AX_X, ALU.add))
                step(nc.vector.tensor_scalar(job_number[:, 1:1 + JOBS], job_expert, -1.0, 0.0, ALU.add, ALU.max))
                nc.vector.tensor_copy(job_regs[:], job_number[0:1, :]).then_inc(jobs_ready, 1)

            def place_jobs():
                for values, result in ((place, job_place), (gate, job_gate)):
                    product = job_tmp[:, 0:TT * JOBS * E].rearrange("p (t j e) -> p t j e", t=TT, j=JOBS)
                    step(nc.vector.tensor_tensor(product, job_is.unsqueeze(1).to_broadcast([P, TT, JOBS, E]),
                                                 values[:].unsqueeze(2).to_broadcast([P, TT, JOBS, E]), ALU.mult))
                    step(nc.vector.tensor_reduce(result, product, AX_X, ALU.add))
                step(nc.vector.tensor_tensor(job_place, job_place, job_base.unsqueeze(1).to_broadcast([P, TT, JOBS]), ALU.subtract))
                product = job_tmp.rearrange("p (j t e) -> p j t e", j=JOBS, t=TILES1)
                step(nc.vector.tensor_tensor(product, job_is.unsqueeze(2).to_broadcast([P, JOBS, TILES1, E]),
                                             bias1[:].rearrange("p (e t) -> p t e", e=E).unsqueeze(1).to_broadcast([P, JOBS, TILES1, E]), ALU.mult))
                step(nc.vector.tensor_reduce(job_bias, product, AX_X, ALU.add))

            def pick_job(k):
                for t in range(TT):
                    nc.vector.tensor_scalar(job_chosen[:, k, t], places, job_place[:, t, k:k + 1], None, ALU.is_equal).then_inc(job_picked, 1)
                    nc.vector.tensor_scalar(job_weighted[:, k, t], places, job_place[:, t, k:k + 1], job_gate[:, t, k:k + 1],
                                            ALU.is_equal, ALU.mult).then_inc(job_picked, 1)

            def copy_tokens(done, tokens, new_hi, new_lo):
                hi, lo = tokens
                nc.vector.tensor_copy(hi, new_hi).then_inc(done, 1)
                for half in range(2):
                    rows = slice(CL * half, CL * (half + 1))
                    nc.vector.tensor_copy(lo[rows, half], new_lo[rows]).then_inc(done, 1)

            def copy_job(k):
                dve.wait_ge(job_gathered, k + 1)
                if k == 0:
                    dve.wait_ge(zeros_job, 1)
                copy_tokens(job_x, tokens_of(E + k), bank[7][:, 0:SLOTS], bank[7][:, SLOTS:2 * SLOTS])
                nc.vector.tensor_copy(job_weightedT[0:SLOTS, k, :], bank[7][0:SLOTS, TOK:2 * TOK]).then_inc(job_x, 1)

            def extra(i, e):
                done = over_chosen[i]
                nc.vector.tensor_scalar(over_place[:], place[:, :, e], -float(i * SLOTS), None, ALU.add).then_inc(done, 1)
                dve.wait_ge(done, OVER_CHOSEN * e + 1)
                for t in range(TT):
                    nc.vector.tensor_scalar(chosen[:, t, 0, :], places, over_place[:, t:t + 1], None, ALU.is_equal).then_inc(done, 1)
                    nc.vector.tensor_scalar(weighted[:, t, 0, :], places, over_place[:, t:t + 1], gate[:, t, e:e + 1],
                                            ALU.is_equal, ALU.mult).then_inc(done, 1)
                dve.wait_ge(over_gathered[i], e + 1)
                copy_tokens(over_x[i], tokens_of(0), bank[0][:, 0:SLOTS], bank[1][:, 0:SLOTS])
                nc.vector.tensor_copy(weightedT[0:SLOTS, 0, :], bank[7][0:SLOTS, 0:TOK]).then_inc(over_x[i], 1)
                stream(0, over[i], steps_of(0, e), "over")
                dve.wait_ge(over[i]["combined"], e + 1)

            def skipped(i, e):
                return [(over_chosen[i], OVER_CHOSEN), (over_x[i], OVER_X), (over[i]["hidden_vec"], len(steps_of(0, e))),
                        (over[i]["y_ready"], 1)]

            def experts(layer):
                dve.wait_ge(scores_psum, (layer + 1) * HEADS)
                for batch in range(2):
                    some = slice(4 * batch, 4 * batch + 4)
                    for t in range(TT):
                        nc.vector.tensor_tensor(chosen[:, t, some], places.unsqueeze(1).to_broadcast([P, 4, SLOTS]),
                                                place[:, t, some].unsqueeze(2).to_broadcast([P, 4, SLOTS]), ALU.is_equal).then_inc(chosen_ready, 1)
                step(nc.vector.tensor_copy(count[:], bank[4][:, TT * E:(TT + 1) * E]))
                step(nc.vector.tensor_copy(counts[0:1, 0:E], count[0:1, :]))
                nc.vector.tensor_reduce(counts[0:1, E:E + 1], count[0:1, :], AX_X, ALU.max).then_inc(counts_ready, 1)
                for batch in range(2):
                    dve.wait_ge(xe_psum, 4 * layer + 2 * batch + 2)
                    for half in range(2):
                        rows = slice(CL * half, CL * (half + 1))
                        nc.vector.tensor_copy(xe_lo[rows, 4 * batch:4 * batch + 4, half, :],
                                              bank[2 * batch + 1][rows, 0:4 * SLOTS].rearrange("p (e s) -> p e s", e=4)).then_inc(xe_vec, 1)
                    if layer == 1 and batch == 0:
                        dve.wait_ge(combT_psum, 1)
                        nc.vector.tensor_copy(combT[0:E, :], bank[5][0:E, P:P + TOK]).then_inc(combT_ready, 1)
                        dve.wait_ge(bias_landed, 32)
                if layer == 0:
                    most = largest_count(dve)
                stream(layer, main[layer], main_steps[layer], "main")
                if layer == 0:
                    dve.wait_ge(main[0]["combined"], E)
                    extra_passes(dve, most, extra, skipped)
                else:
                    def job(k):
                        if k > 0:
                            pick_job(k)
                            copy_job(k)
                        stream(1, main[1], steps_of(1, E + k), "job")

                    jobs(dve, job, lambda k: dve.wait_ge(main[1]["combined"], E + k))

            dve.wait_ge(x_landed, 16)
            norm(0)
            dve.wait_ge(par_landed, 16)
            dve.wait_ge(const_landed, 16)
            attend(0)
            norm(1)
            round_xn(0)
            route(0)
            experts(0)
            dve.wait_ge(acc_ready, 1)
            for t in range(TT):
                nc.vector.tensor_tensor(x[:, t, :], acc[:, t], bank[4][:, t * C:(t + 1) * C], ALU.add).then_inc(moe_done, 1)
            norm(2)
            attend(1)
            norm(3)
            round_xn(1)
            route(1)
            experts(1)
            for t in range(TT):
                nc.vector.tensor_tensor(x[:, t, :], x[:, t, :], bank[4][:, t * C:(t + 1) * C], ALU.add).then_inc(x_ready, 2)

        @block.tensor
        def _(pe):
            def keep_clock(n, b=3):
                pe.wait_ge(ones_set, 3)
                for _ in range(n):
                    nc.tensor.matmul(bank[b][:, 0:P], ones[:], ones[:], start=True, stop=True)

            def norm_T(n):
                if n % 2 == 0:
                    pe.wait_ge(xn_ready, xn_count(n))
                if n == 2:
                    pe.wait_ge(moe_done, TT)
                for t in range(TT):
                    cols = slice(t * P, (t + 1) * P)
                    if n % 2 == 0:
                        nc.tensor.transpose(bank[6][:, cols], xn[:, t, 0:P], ident)
                        last = nc.tensor.transpose(bank[7][0:CL, cols], xn[:, t, P:C], ident)
                    else:
                        pe.wait_ge(x_added, TT * (n // 2) + t + 1)
                        nc.tensor.transpose(bank[6][:, cols], x[:, t, 0:P], ident)
                        last = nc.tensor.transpose(bank[7][0:CL, cols], x[:, t, P:C], ident)
                last.then_inc(xnT_psum, 1)
                pe.wait_ge(xnT_act, n + 1)
                pe.wait_ge(xnT_vec, n + 1)

            def project(out_ap, cols):
                nc.tensor.matmul(out_ap, att_hi[:, cols], xnT[:, 0, :], start=True, stop=False)
                return nc.tensor.matmul(out_ap, att_lo[0:CL, cols], xnT[0:CL, 1, :], start=False, stop=True)

            def project_tokens(out_ap, t, cols):
                tok = slice(t * P, (t + 1) * P)
                nc.tensor.matmul(out_ap, xnT[:, 0, tok], att_hi[:, cols], start=True, stop=False)
                return nc.tensor.matmul(out_ap, xnT[0:CL, 1, tok], att_lo[0:CL, cols], start=False, stop=True)

            def scores(layer, pair):
                heads = (2 * pair, 2 * pair + 1)
                g = heads[0] // HB
                pe.wait_ge(q_split, HG * layer + g + 1)
                pe.wait_ge(k_rounded, HG * layer + g + 1)
                pe.wait_ge(k_split, HG * layer + g + 1)
                if layer == 0:
                    pe.wait_ge(rel_split, g + 1)
                for h in heads:
                    if layer * HEADS + h >= HB:
                        pe.wait_ge(probs_ready, TT * (layer * HEADS + h - HB + 1))
                terms = [(q_parts, k_hi), (q_parts, k_lo)]
                if layer == 0:
                    terms += [(rel_hi, None), (rel_lo, None)]
                for t in range(TT):
                    for i, (left, right) in enumerate(terms):
                        for h in heads:
                            b = h % HB
                            rows = slice(SLOT * b, SLOT * (b + 1))
                            last = nc.tensor.matmul(bank[b][:, t * TOK:(t + 1) * TOK], left[rows, g, t * P:(t + 1) * P],
                                                    right[rows, g, :] if right is not None else onehot_r[rows, :],
                                                    start=i == 0, stop=i == len(terms) - 1, tile_position=(SLOT * b, 0))
                            if t == TT - 1 and i == len(terms) - 1:
                                last.then_inc(scores_psum, 1)

            def turn(layer, h):
                head = layer * HEADS + h
                pe.wait_ge(probs_ready, TT * (head + 1))
                if head >= 2:
                    wait_probsT(pe, head - 2)
                for k in range(TT):
                    for t in range(TT):
                        at = k * TOK + t * P
                        last = nc.tensor.transpose(bank[4 + head % 2][:, at:at + P], probs[:, h % HB, t, k * P:(k + 1) * P], ident)
                last.then_inc(probsT_psum, 1)

            def weigh(layer, h):
                head = layer * HEADS + h
                wait_probsT(pe, head)
                g, b = h // HB, h % HB
                if b == 0 and g >= 2:
                    pe.wait_ge(o_copied, HG * layer + g - 1)
                for k in range(TT):
                    last = nc.tensor.matmul(bank[6 + g % 2][SLOT * b:SLOT * (b + 1), 0:TOK], v1[:, k, h, :],
                                            probsT[:, head % TRING, k, :], start=k == 0, stop=k == TT - 1,
                                            tile_position=(0, SLOT * b))
                last.then_inc(o_psum, 1)

            def attend(layer):
                pe.wait_ge(att_landed[layer], 32)
                for g in range(HG):
                    last = project(bank[g // 2][:, (g % 2) * TOK:(g % 2 + 1) * TOK],
                                   slice(W_QK + QK + g * P, W_QK + QK + (g + 1) * P))
                last.then_inc(k_psum, 1)
                for g in range(HG):
                    last = project(bank[2 + g // 2][:, (g % 2) * TOK:(g % 2 + 1) * TOK], slice(W_QK + g * P, W_QK + (g + 1) * P))
                last.then_inc(q_psum, 1)
                for t in range(TT):
                    last = project_tokens(bank[4][:, t * C:(t + 1) * C], t, slice(W_V, W_V + C))
                last.then_inc(v_psum, 1)
                if layer == 0:
                    pe.wait_ge(rel_landed, 32)
                    pe.wait_ge(q_ready, HG)
                    for axis, banks in enumerate(((5, 6), (7, 3))):
                        order = "p g (r c) -> p r g c" if axis == 0 else "p g (r c) -> p c g r"
                        lines = qT[:].rearrange(order, c=GRID)
                        for i in range(GRID):
                            if (axis, i) == (1, GRID // 2):
                                pe.wait_ge(q_rounded, HG)
                            window = rel_t[:, axis, GRID - 1 - i:GRID - 1 - i + P]
                            at = (i % 8) * HG * GRID
                            last = nc.tensor.matmul(bank[banks[i // 8]][:, at:at + HG * GRID], window, lines[:, i],
                                                    start=True, stop=True)
                        last.then_inc(rel_psum, 1)
                pe.wait_ge(k_ready, HG * (layer + 1))
                pe.wait_ge(ones_set, 4)
                keep_clock(KEEP_SCORES[layer], 1)
                scores(layer, 0)
                pe.wait_ge(q_ready, HG * (layer + 1))
                pe.wait_ge(q_rounded, HG * (layer + 1))
                if layer == 0:
                    pe.wait_ge(rel_ready, 2 * HG)
                scores(layer, 1)
                pe.wait_ge(v_ready, TT * (layer + 1))
                for h in range(HEADS):
                    if h % 2 == 0 and 0 < h and h + 2 < HEADS:
                        scores(layer, h // 2 + 1)
                    turn(layer, h)
                    if h >= 2:
                        weigh(layer, h - 2)
                pe.wait_ge(o_copied, HG * layer + 2)
                for t in range(TT):
                    for g in range(2):
                        last = nc.tensor.transpose(bank[t][:, g * P:(g + 1) * P], qT[:, g, t * P:(t + 1) * P], ident)
                last.then_inc(o_turned, 1)
                weigh(layer, HEADS - 2)
                weigh(layer, HEADS - 1)
                nc.tensor.matmul(bank[5][:, TT * E:(TT + 1) * E], ones[:], att_hi[:, W_ROUTER:W_ROUTER + E], start=True, stop=False)
                nc.tensor.matmul(bank[5][:, TT * E:(TT + 1) * E], ones[0:CL, :], att_lo[0:CL, W_ROUTER:W_ROUTER + E],
                                 start=False, stop=True).then_inc(router_sum_psum, 1)
                pe.wait_ge(o_ready, TT * (2 * layer + 1))
                for t in range(TT):
                    last = nc.tensor.transpose(bank[7][:, t * P:(t + 1) * P], o_tok[:, t, 0:P], ident)
                last.then_inc(oT_psum, 1)
                pe.wait_ge(o_copied, HG * (layer + 1))
                for t in range(TT):
                    last = nc.tensor.transpose(bank[t][:, 2 * P:3 * P], qT[:, 2, t * P:(t + 1) * P], ident)
                last.then_inc(o_turned, 1)
                pe.wait_ge(oT_ready, 2 * layer + 1)
                for t in range(TT):
                    nc.tensor.matmul(bank[4][:, t * C:(t + 1) * C], oT[:, 0, t * P:(t + 1) * P], att_hi[:, W_OUT:W_OUT + C],
                                     start=t == 0, stop=False, skip_group_check=True)
                pe.wait_ge(o_ready, TT * (2 * layer + 2))
                for t in range(TT):
                    last = nc.tensor.transpose(bank[2][0:CL, t * P:(t + 1) * P], o_tok[:, t, P:C], ident)
                last.then_inc(oT_psum, 1)
                pe.wait_ge(oT_ready, 2 * layer + 2)
                for t in range(TT):
                    last = nc.tensor.matmul(bank[4][:, t * C:(t + 1) * C], oT[0:CL, 1, t * P:(t + 1) * P], att_lo[0:CL, W_OUT:W_OUT + C],
                                            start=False, stop=True, skip_group_check=True)
                last.then_inc(proj_psum, 1)

            def router(layer):
                for t in range(TT):
                    last = project_tokens(bank[5][:, t * E:(t + 1) * E], t, slice(W_ROUTER, W_ROUTER + E))
                last.then_inc(logit_psum, 1)
                keep_clock(KEEP_ROUTE)

            def places_of(layer):
                pe.wait_ge(picked, TT * (layer + 1))
                pe.wait_ge(ones_set, 6)
                both = mask[:].rearrange("p t e -> p (t e)")
                nc.tensor.matmul(bank[4][:, 0:TT * E], upper_b[:], both, start=True, stop=False, skip_group_check=True)
                nc.tensor.matmul(bank[4][:, E:2 * E], ones_b[:], mask[:, 0], start=False, stop=True, skip_group_check=True)
                for t in range(TT):
                    last = nc.tensor.matmul(bank[4][:, 2 * E:3 * E], ones_b[:], mask[:, t], start=False, stop=t == TT - 1,
                                            skip_group_check=True)
                last.then_inc(place_psum, 1)
                keep_clock(KEEP_PLACE)

            def gather(out_ap, c, tokens, ready=None):
                for i, part in enumerate((xn_hi, xn_lo)):
                    for t in range(TT):
                        if ready is not None and i == 0:
                            pe.wait_ge(chosen_ready, ready + t + 1)
                        last = nc.tensor.matmul(out_ap, part[:, t, c * P:(c + 1) * P], tokens(t),
                                                start=i == 0 and t == 0, stop=i == 1 and t == TT - 1)
                return last

            def first_products(layer, n, tokens, begin):
                e, t, m = steps_of_layer[layer][n]
                hi, lo = tokens
                if layer == 0:
                    long, short = (t * P, HID0[e] + t * P), 2 * HID0[e] + t * P
                else:
                    long, short = (t * P, (STEPS1 + t) * P), HID1 + t * P
                tile = up_bank(n)[0:m]
                for u in range(2):
                    nc.tensor.matmul(tile[:, u], w0[:, begin + long[u]:begin + long[u] + m], hi, start=u == 0, stop=False,
                                     skip_group_check=True)
                return nc.tensor.matmul(tile.rearrange("p u s -> p (u s)"), w0[:, begin + short:begin + short + m],
                                        lo.rearrange("p u s -> p (u s)"), start=False, stop=True, skip_group_check=True)

            def down(layer, sems, n, begin):
                e, t, m = steps_of_layer[layer][n]
                if t == 0 and e >= 2:
                    pe.wait_ge(sems["y_ready"], e - 1)
                wait_hidden(pe, layer, sems, n)
                for u in range(layer + 1):
                    at = 3 * HID0[e] + t * C if layer == 0 else HID1 + HID1 // 2 + (t + u * STEPS1) * C
                    ins = nc.tensor.matmul(y_bank(e)[0:SLOTS, 0:C], hidden[0:m, n % RING, u], w0[0:m, begin + at:begin + at + C],
                                           start=t == 0 and u == 0, stop=n + 1 == first_step[layer][e + 1] and u == layer)
                ins.then_inc(sems["hidden_used"], 1)

            def combine(layer, sems, e, turned, first, last):
                pe.wait_ge(sems["y_ready"], e + 1)
                for t in range(TT):
                    ins = nc.tensor.matmul(bank[4][:, t * C:(t + 1) * C], turned[0:SLOTS, t * P:(t + 1) * P], y_out[0:SLOTS, e % 2, :],
                                           start=first and t == 0, stop=last, skip_group_check=True)
                ins.then_inc(sems["combined"], 1)

            def turn_weighted(layer, pair):
                for e in (2 * pair, 2 * pair + 1):
                    pe.wait_ge(weighted_ready, TT * (E * layer + e + 1))
                    for t in range(TT):
                        at = (e % 2) * TOK + t * P
                        last = nc.tensor.transpose(weightedT_bank(pair)[0:SLOTS, at:at + P], weighted[:, t, e, :], ident)
                last.then_inc(weightedT_psum, 1)

            def experts(layer):
                for batch in range(2):
                    pe.wait_ge(xn_rounded, layer + 1)
                    pe.wait_ge(xn_split, layer + 1)
                    for c in range(2):
                        gather(bank[2 * batch + c][:, 0:4 * SLOTS], c, lambda t: chosen[:, t, 4 * batch:4 * batch + 4].rearrange("p e s -> p (e s)"),
                               TT * (2 * layer + batch)).then_inc(xe_psum, 1)
                if layer == 1:
                    pe.wait_ge(gate_ready, 2)
                    for t in range(TT):
                        last = nc.tensor.transpose(bank[5][0:E, P + t * P:P + (t + 1) * P], gate[:, t, :], ident)
                    last.then_inc(combT_psum, 1)
                sems, lag = main[layer], LAG[layer]
                begin = OFF0 if layer == 0 else [e * SIZE1 for e in range(E)]
                landed = (e0_landed, e1_landed)[layer]
                for n in main_steps[layer]:
                    e, t, m = steps_of_layer[layer][n]
                    if t == 0:
                        pe.wait_ge(landed[e], 16)
                    if n == 0:
                        pe.wait_ge(zeros_set, 2)
                    if n == 0 or n == 2:
                        pe.wait_ge(xe_act, 2 * layer + (1 if n == 0 else 2))
                        pe.wait_ge(xe_vec, 4 * layer + (2 if n == 0 else 4))
                    if n >= DEPTH:
                        wait_hidden(pe, layer, sems, n - DEPTH)
                    if n == lag:
                        pe.wait_ge(place_ready, layer + 1)
                        pe.wait_ge(counts_ready, layer + 1)
                        if layer == 1:
                            pe.wait_ge(combT_ready, 1)
                            pe.wait_ge(bias_landed, 32)
                            for i in range(TT):
                                nc.tensor.matmul(bank[4][:, i * C:(i + 1) * C], combT[0:E, i * P:(i + 1) * P], bias2[0:E, :],
                                                 start=i == 0, stop=False, skip_group_check=True)
                    if (e, t) == (1, 0):
                        pe.wait_ge(weightedT_act, 2 * layer + 1)
                    first_products(layer, n, tokens_of(e), begin[e]).then_inc(sems["up_psum"], 1)
                    if n >= lag:
                        down(layer, sems, n - lag, begin[steps_of_layer[layer][n - lag][0]])
                    if t == lag + 1 and e >= 1:
                        combine(layer, sems, e - 1, weightedT[:, e - 1], layer == 0 and e == 1, False)
                    if (e, t) in PAIR_AT:
                        pair = PAIR_AT.index((e, t))
                        if pair >= 2:
                            pe.wait_ge(weightedT_vec, 2 * layer + pair - 1)
                        turn_weighted(layer, pair)
                    if (e, t) == (6, 0):
                        pe.wait_ge(weightedT_act, 2 * layer + 2)
                    if layer == 1 and (e, t) == GATHER_JOB_AT:
                        gather_job(0)
                for n in main_steps[layer][-lag:]:
                    down(layer, sems, n, begin[E - 1])
                if layer == 0:
                    combine(0, sems, E - 1, weightedT[:, E - 1], False, True)
                    extra_passes(pe, largest_count(pe), extra, skipped)
                else:
                    jobs(pe, job, lambda k: combine_last(E + k - 1))

            def extra(i, e):
                sems = over[i]
                pe.wait_ge(over_chosen[i], OVER_CHOSEN * (e + 1))
                for c in range(2):
                    gather(bank[c][:, 0:SLOTS], c, lambda t: chosen[:, t, 0])
                for t in range(TT):
                    last = nc.tensor.transpose(bank[7][0:SLOTS, t * P:(t + 1) * P], weighted[:, t, 0, :], ident)
                last.then_inc(over_gathered[i], 1)
                pe.wait_ge(over_x[i], OVER_X * (e + 1))
                ns = steps_of(0, e)
                for n in ns:
                    if n >= DEPTH:
                        wait_hidden(pe, 0, sems, n - DEPTH)
                    first_products(0, n, tokens_of(0), OFF0[e]).then_inc(sems["up_psum"], 1)
                    if n - LAG[0] in ns:
                        down(0, sems, n - LAG[0], OFF0[e])
                for n in ns[-LAG[0]:]:
                    down(0, sems, n, OFF0[e])
                combine(0, sems, e, weightedT[:, 0], False, True)

            def skipped(i, e):
                k = len(steps_of(0, e))
                return [(over_gathered[i], 1), (over[i]["up_psum"], k), (over[i]["hidden_used"], k), (over[i]["combined"], 1)]

            def gather_job(k):
                pe.wait_ge(job_picked, 2 * TT * (k + 1))
                if k == 0:
                    pe.wait_ge(weightedT_act, 4)
                for c in range(2):
                    gather(bank[7][:, c * SLOTS:(c + 1) * SLOTS], c, lambda t: job_chosen[:, k, t])
                for t in range(TT):
                    last = nc.tensor.transpose(bank[7][0:SLOTS, TOK + t * P:TOK + (t + 1) * P], job_weighted[:, k, t], ident)
                last.then_inc(job_gathered, 1)

            def combine_last(e):
                combine(1, main[1], e, weightedT[:, e] if e < E else job_weightedT[:, e - E], False, True)

            def job(k):
                sems, ns = main[1], steps_of(1, E + k)
                begin = job_weights_at[k % JOB_ROOMS]
                if k > 0:
                    gather_job(k)
                pe.wait_ge(job_x, OVER_X * (k + 1))
                pe.wait_ge(job_landed[k], 16)
                for n in ns:
                    wait_hidden(pe, 1, sems, n - DEPTH)
                    first_products(1, n, tokens_of(E + k), begin).then_inc(sems["up_psum"], 1)
                    if n - LAG[1] in ns:
                        down(1, sems, n - LAG[1], begin)
                combine_last(E + k - 1)
                for n in ns[-LAG[1]:]:
                    down(1, sems, n, begin)

            keep_clock(KEEP_START)
            pe.wait_ge(const_landed, 16)
            norm_T(0)
            attend(0)
            norm_T(1)
            router(0)
            places_of(0)
            experts(0)
            keep_clock(KEEP_NORM)
            norm_T(2)
            attend(1)
            norm_T(3)
            router(1)
            places_of(1)
            experts(1)


def lay_out(inputs):
    f = {k: np.asarray(v) for k, v in inputs.items()}

    def heads_apart(w):
        w = w.reshape(w.shape[0], HEADS, 1, HD)
        return np.concatenate([w, w], axis=2).reshape(w.shape[0], QK)

    def layer_weights(qkv, w_out, router):
        q, k, v = qkv[:, 0:C], qkv[:, C:2 * C], qkv[:, 2 * C:3 * C]
        return np.concatenate([heads_apart(q), heads_apart(k), v, w_out, router], axis=1)

    def layer_params(b_qkv, b_out, b_gate):
        apart = heads_apart(b_qkv[None, 0:2 * C].reshape(2, C)).reshape(2 * HG, P).T
        rows = np.concatenate([b_qkv[2 * C:3 * C], b_out, b_gate])
        return np.concatenate([apart, np.broadcast_to(rows, (P, rows.size))], axis=1)

    w = np.stack([
        layer_weights(f["L0_conv_w_qkv"], f["L0_conv_w_o"], f["L0_ffn_router_W"].T),
        layer_weights(f["L1_conv_qkv_w"].T, f["L1_conv_proj_w"].T, f["L1_ffn_gate_w"].T)])
    no_bias = np.zeros((E,), np.float32)
    params = np.stack([layer_params(f["L0_conv_b_qkv"], f["L0_conv_b_o"], no_bias),
                       layer_params(f["L1_conv_qkv_b"], f["L1_conv_proj_b"], f["L1_ffn_gate_b"])], axis=1)

    rel = np.zeros((HB, SLOT, 2, REL_W), np.float32)
    for axis, name in enumerate(("L0_conv_rel_pos_h", "L0_conv_rel_pos_w")):
        for b in range(HB):
            at = SLOT * b + GRID * axis
            rel[b, 0:HD, axis, at:at + REL] = f[name][::-1].T
    key = np.arange(TOK)
    slot = np.arange(P) % SLOT
    onehot = np.where(slot[:, None] < GRID, key // GRID == slot[:, None], key % GRID == slot[:, None] - GRID)
    ranks = np.broadcast_to(np.arange(E, 0, -1), (P, E))
    masks = np.stack([slot < GRID, slot >= GRID, -1.0 * (slot >= GRID)], axis=1)
    numbers = np.arange(P)
    const = np.concatenate([np.eye(P), numbers[:, None] < numbers, np.broadcast_to(numbers + 1, (P, P)),
                            np.full((P, 1), -0.5), masks, ranks, onehot], axis=1).astype(np.float32)

    blocks = []
    for e in range(E):
        gate, up, down = f[f"L0_ffn_gate_W_{e}"].T, f[f"L0_ffn_up_W_{e}"].T, f[f"L0_ffn_down_W_{e}"].T
        down = np.pad(down, ((0, TILES0[e] * P - HID0[e]), (0, 0))).reshape(TILES0[e], P, C)
        blocks += [gate[0:P], up[0:P], np.concatenate([gate[P:C], up[P:C]]), down.transpose(1, 0, 2).reshape(P, -1)]
    experts0 = np.concatenate(blocks, axis=1)
    w1 = f["L1_ffn_w1"].transpose(2, 0, 1)
    lo = w1[P:C].reshape(CL, E, 2, HID1 // 2).transpose(2, 0, 1, 3).reshape(P, E, HID1 // 2)
    w2 = f["L1_ffn_w2"].transpose(0, 2, 1).reshape(E, TILES1, P, C).transpose(2, 0, 1, 3).reshape(P, E, TILES1 * C)
    experts1 = np.concatenate([w1[0:P], lo, w2], axis=2)
    arrays = {
        "x": f["x"].reshape(TOK, C), "weights_hi": w[:, 0:P], "weights_lo": w[:, P:C], "params": params,
        "rel": rel.reshape(P, 2, REL_W), "const": const, "experts0": experts0, "experts1": experts1,
        "bias1": f["L1_ffn_b1"].reshape(E * TILES1, P).T, "bias2": f["L1_ffn_b2"],
    }
    return {k: np.ascontiguousarray(v, dtype=np.float32) for k, v in arrays.items()}


def kernel(**inputs):
    import concourse.bacc as bacc
    from concourse.bass_utils import run_bass_kernel_spmd

    nc = bacc.Bacc("TRN2", target_bir_lowering=False, num_devices=1)
    arrays = lay_out(inputs)
    args = [nc.dram_tensor(f"{name}_dram", a.shape, F32, kind="ExternalInput").ap() for name, a in arrays.items()]
    out = nc.dram_tensor("out_dram", (TOK, C), F32, kind="ExternalOutput").ap()
    metaformer_kernel(nc, *args, out)
    result = run_bass_kernel_spmd(nc, [{f"{name}_dram": a for name, a in arrays.items()}], core_ids=[0])
    return result.results[0]["out_dram"].reshape(1, GRID, GRID, C)
```
